# Optimizing a Trainium2 kernel written in Bass

```python
import numpy as np
import jax
import jax.numpy as jnp

def _softmax(x, axis=-1):
    return jax.nn.softmax(x, axis=axis)

def _gelu(x):
    return jax.nn.gelu(x, approximate=True)

def _silu(x):
    return jax.nn.silu(x)

def _sigmoid(x):
    return jax.nn.sigmoid(x)

def _layernorm(x, axis=-1, eps=1e-05):
    m = jnp.mean(x, axis=axis, keepdims=True)
    v = jnp.var(x, axis=axis, keepdims=True)
    return (x - m) / jnp.sqrt(v + eps)

def _scatter_add(tgt, idx, src, axis=0):
    return tgt.at[idx].add(src)

def _segment_sum(src, seg, n):
    return jax.ops.segment_sum(src, seg, n)
kernel_name = 'mk_xattn_ffn_d2_seqx_r4_2155e6'

def setup_inputs(seed: int=0):
    np.random.seed(seed)
    _w = jnp.asarray

    def _rec_inputs():
        import jax
        import jax.numpy as jnp
        _rk = jax.random.key(seed)
        x = -0.0002928 + 1 * jax.random.normal(jax.random.fold_in(_rk, 1), (8, 256, 256), jnp.float32)
        _lenS = 256 - jax.random.randint(jax.random.fold_in(_rk, 7), (8,), 0, max(1, 256 // 4) + 1, jnp.int32)
        _lenS2 = 256 - jax.random.randint(jax.random.fold_in(_rk, 8), (8,), 0, max(1, 256 // 4) + 1, jnp.int32)
        _ctx_1024P = jax.random.normal(jax.random.fold_in(_rk, 11), (8, 16, 256), jnp.float32)
        _ctx_1024c = jax.random.dirichlet(jax.random.fold_in(_rk, 511), 0.3 * jnp.ones((16,), jnp.float32), (8, 256))
        _ctx_1024t = jnp.einsum('bsk,bkd->bsd', _ctx_1024c, _ctx_1024P)
        _ctx_1024t = _ctx_1024t * jax.lax.rsqrt(jnp.mean(jnp.square(_ctx_1024t)) + 1e-12) * 0.953939
        ctx_1024 = 4.13588e-05 + 0.999923 * (_ctx_1024t + 0.3 * jax.random.normal(jax.random.fold_in(_rk, 611), (8, 256, 256), jnp.float32))
        _validS = jnp.arange(256)[None, :] < _lenS[:, None]
        _validS2 = jnp.arange(256)[None, :] < _lenS2[:, None]
        _causal = jnp.tril(jnp.ones((256, 256), dtype=bool))
        mask_Bx1x1xS2_ff0 = jnp.where(jnp.ones((8, 1, 1, 256), dtype=bool), 0.0, -1000000000.0).astype(jnp.float32)
        return (x, ctx_1024, mask_Bx1x1xS2_ff0)
    x, ctx_1024, mask_Bx1x1xS2_ff0 = _rec_inputs()

    def _L0_xattn_setup():
        import jax, jax.numpy as jnp
        import numpy as np
        H = 16
        D = 256
        F = 1024
        LN_EPS = 1e-05

        def _glorot(key, shape):
            fan_in, fan_out = (shape[0], shape[1])
            lim = np.sqrt(6.0 / (fan_in + fan_out))
            return jax.random.uniform(key, shape, jnp.float32, -lim, lim)

        def _split_heads(x):
            b, l, _ = x.shape
            return x.reshape(b, l, H, D // H)

        def _mha(x, ctx, mask, qw, qb, kw, kb, vw, vb):
            q = _split_heads(x @ qw + qb)
            k = _split_heads(ctx @ kw + kb)
            v = _split_heads(ctx @ vw + vb)
            scores = jnp.einsum('bqhd,bkhd->bhqk', q, k) / np.sqrt(D // H).astype(np.float32)
            if mask is not None:
                scores = scores + mask
            probs = jax.nn.softmax(scores, axis=-1)
            out = jnp.einsum('bhqk,bkhd->bqhd', probs, v)
            return out.reshape(x.shape[0], x.shape[1], D)

        def _self_output(h, residual, w, b, g, be):
            h = h @ w + b
            h = h + residual
            mu = jnp.mean(h, axis=-1, keepdims=True)
            var = jnp.mean(jnp.square(h - mu), axis=-1, keepdims=True)
            return (h - mu) * jax.lax.rsqrt(var + LN_EPS) * g + be
        key = jax.random.key(seed)
        ks = jax.random.split(key, 16)
        inp = {'input_tensor': jax.random.normal(ks[0], (4, 256, D), jnp.float32), 'ctx_tensor': jax.random.normal(ks[1], (4, 512, D), jnp.float32), 'ctx_attn_mask': jnp.zeros((4, 1, 1, 512), jnp.float32), 'cq_w': _glorot(ks[2], (D, D)), 'cq_b': jnp.zeros((D,)), 'ck_w': _glorot(ks[3], (D, D)), 'ck_b': jnp.zeros((D,)), 'cv_w': _glorot(ks[4], (D, D)), 'cv_b': jnp.zeros((D,)), 'co_w': _glorot(ks[5], (D, D)), 'co_b': jnp.zeros((D,)), 'co_g': jnp.ones((D,)), 'co_be': jnp.zeros((D,)), 'sq_w': _glorot(ks[6], (D, D)), 'sq_b': jnp.zeros((D,)), 'sk_w': _glorot(ks[7], (D, D)), 'sk_b': jnp.zeros((D,)), 'sv_w': _glorot(ks[8], (D, D)), 'sv_b': jnp.zeros((D,)), 'so_w': _glorot(ks[9], (D, D)), 'so_b': jnp.zeros((D,)), 'so_g': jnp.ones((D,)), 'so_be': jnp.zeros((D,)), 'fi_w': _glorot(ks[10], (D, F)), 'fi_b': jnp.zeros((F,)), 'fo_w': _glorot(ks[11], (F, D)), 'fo_b': jnp.zeros((D,)), 'fo_g': jnp.ones((D,)), 'fo_be': jnp.zeros((D,))}
        return inp
    _L0_xattn_all = _L0_xattn_setup()
    _L0_xattn_in = {k: v for k, v in _L0_xattn_all.items() if k in ('cq_w', 'cq_b', 'ck_w', 'ck_b', 'cv_w', 'cv_b', 'co_w', 'co_b', 'co_g', 'co_be', 'sq_w', 'sq_b', 'sk_w', 'sk_b', 'sv_w', 'sv_b', 'so_w', 'so_b', 'so_g', 'so_be', 'fi_w', 'fi_b', 'fo_w', 'fo_b', 'fo_g', 'fo_be')}
    del _L0_xattn_all

    def _L0_ffn_setup():
        import math
        import jax, jax.numpy as jnp
        import numpy as np
        NUM_EXPERTS = 8
        TOP_K = 2
        CAPACITY_FACTOR = 1.0
        B, S, H, I = (4, 512, 256, 1024)
        key = jax.random.key(seed)
        k_x, k_rw, k_wi, k_wo = jax.random.split(key, 4)
        x = jax.random.normal(k_x, (B, S, H), dtype=jnp.float32)
        lim = math.sqrt(6.0 / (H + NUM_EXPERTS))
        router_w = jax.random.uniform(k_rw, (NUM_EXPERTS, H), minval=-lim, maxval=lim, dtype=jnp.float32)
        router_b = jnp.zeros((NUM_EXPERTS,), dtype=jnp.float32)
        experts_inter = jax.random.normal(k_wi, (NUM_EXPERTS - 1, H, I), dtype=jnp.float32) / math.sqrt(H)
        experts_out = jax.random.normal(k_wo, (NUM_EXPERTS - 1, I, H), dtype=jnp.float32) / math.sqrt(I)
        return {'x': x, 'router_w': router_w, 'router_b': router_b, 'experts_inter': experts_inter, 'experts_out': experts_out}
    _L0_ffn_all = _L0_ffn_setup()
    _L0_ffn_in = {k: v for k, v in _L0_ffn_all.items() if k in ('router_w', 'router_b', 'experts_inter', 'experts_out')}
    del _L0_ffn_all

    def _L1_xattn_setup():
        import jax, jax.numpy as jnp
        import numpy as np
        D_MODEL = 256
        NUM_HEADS = 16
        D_K = D_MODEL // NUM_HEADS

        def _mha(Q, K, V, W_q, b_q, W_k, b_k, W_v, b_v, W_o, b_o):
            B, L, _ = Q.shape
            H, dk = (NUM_HEADS, D_K)
            q = (Q @ W_q.T + b_q).reshape(B, L, H, dk).transpose(0, 2, 1, 3)
            k = (K @ W_k.T + b_k).reshape(B, L, H, dk).transpose(0, 2, 1, 3)
            v = (V @ W_v.T + b_v).reshape(B, L, H, dk).transpose(0, 2, 1, 3)
            scale = jnp.sqrt(jnp.float32(dk))
            scores = jnp.einsum('bhqd,bhkd->bhqk', q, k) / scale
            attn = jax.nn.softmax(scores, axis=-1)
            out = jnp.einsum('bhqk,bhkd->bhqd', attn, v)
            out = out.transpose(0, 2, 1, 3).reshape(B, L, H * dk)
            return out @ W_o.T + b_o
        key = jax.random.key(seed)
        ks = jax.random.split(key, 11)
        B, L = (2, 512)
        s = 1.0 / np.sqrt(D_MODEL)
        inp = {'Q': jax.random.normal(ks[0], (B, L, D_MODEL), jnp.float32), 'K': jax.random.normal(ks[1], (B, L, D_MODEL), jnp.float32), 'V': jax.random.normal(ks[2], (B, L, D_MODEL), jnp.float32), 'W_q': jax.random.normal(ks[3], (D_MODEL, D_MODEL), jnp.float32) * s, 'b_q': jax.random.normal(ks[4], (D_MODEL,), jnp.float32) * s, 'W_k': jax.random.normal(ks[5], (D_MODEL, D_MODEL), jnp.float32) * s, 'b_k': jax.random.normal(ks[6], (D_MODEL,), jnp.float32) * s, 'W_v': jax.random.normal(ks[7], (D_MODEL, D_MODEL), jnp.float32) * s, 'b_v': jax.random.normal(ks[8], (D_MODEL,), jnp.float32) * s, 'W_o': jax.random.normal(ks[9], (D_MODEL, D_MODEL), jnp.float32) * s, 'b_o': jax.random.normal(ks[10], (D_MODEL,), jnp.float32) * s}
        return inp
    _L1_xattn_all = _L1_xattn_setup()
    _L1_xattn_in = {k: v for k, v in _L1_xattn_all.items() if k in ('W_q', 'b_q', 'W_k', 'b_k', 'W_v', 'b_v', 'W_o', 'b_o')}
    del _L1_xattn_all

    def _L1_ffn_setup():
        import jax, jax.numpy as jnp
        import numpy as np
        CAPACITY_FACTOR = 0.5
        key = jax.random.key(seed)
        ks = jax.random.split(key, 5)
        B, S, D, F = (4, 1024, 256, 1024)
        scale_in = 1.0 / np.sqrt(D)
        scale_ff = 1.0 / np.sqrt(F)
        return {'hidden_states': jax.random.normal(ks[0], (B, S, D), dtype=jnp.float32), 'w_router': jax.random.normal(ks[1], (D,), dtype=jnp.float32) * scale_in, 'W1': jax.random.normal(ks[2], (D, F), dtype=jnp.float32) * scale_in, 'b1': jnp.zeros((F,), dtype=jnp.float32), 'W2': jax.random.normal(ks[3], (F, D), dtype=jnp.float32) * scale_ff, 'b2': jnp.zeros((D,), dtype=jnp.float32)}
    _L1_ffn_all = _L1_ffn_setup()
    _L1_ffn_in = {k: v for k, v in _L1_ffn_all.items() if k in ('w_router', 'W1', 'b1', 'W2', 'b2')}
    del _L1_ffn_all
    return {'x': x, 'ctx_1024': ctx_1024, 'mask_Bx1x1xS2_ff0': mask_Bx1x1xS2_ff0, 'L0_xattn_cq_w': _L0_xattn_in['cq_w'], 'L0_xattn_cq_b': _L0_xattn_in['cq_b'], 'L0_xattn_ck_w': _L0_xattn_in['ck_w'], 'L0_xattn_ck_b': _L0_xattn_in['ck_b'], 'L0_xattn_cv_w': _L0_xattn_in['cv_w'], 'L0_xattn_cv_b': _L0_xattn_in['cv_b'], 'L0_xattn_co_w': _L0_xattn_in['co_w'], 'L0_xattn_co_b': _L0_xattn_in['co_b'], 'L0_xattn_co_g': _L0_xattn_in['co_g'], 'L0_xattn_co_be': _L0_xattn_in['co_be'], 'L0_xattn_sq_w': _L0_xattn_in['sq_w'], 'L0_xattn_sq_b': _L0_xattn_in['sq_b'], 'L0_xattn_sk_w': _L0_xattn_in['sk_w'], 'L0_xattn_sk_b': _L0_xattn_in['sk_b'], 'L0_xattn_sv_w': _L0_xattn_in['sv_w'], 'L0_xattn_sv_b': _L0_xattn_in['sv_b'], 'L0_xattn_so_w': _L0_xattn_in['so_w'], 'L0_xattn_so_b': _L0_xattn_in['so_b'], 'L0_xattn_so_g': _L0_xattn_in['so_g'], 'L0_xattn_so_be': _L0_xattn_in['so_be'], 'L0_xattn_fi_w': _L0_xattn_in['fi_w'], 'L0_xattn_fi_b': _L0_xattn_in['fi_b'], 'L0_xattn_fo_w': _L0_xattn_in['fo_w'], 'L0_xattn_fo_b': _L0_xattn_in['fo_b'], 'L0_xattn_fo_g': _L0_xattn_in['fo_g'], 'L0_xattn_fo_be': _L0_xattn_in['fo_be'], 'L0_ffn_router_w': _L0_ffn_in['router_w'], 'L0_ffn_router_b': _L0_ffn_in['router_b'], 'L0_ffn_experts_inter': _L0_ffn_in['experts_inter'], 'L0_ffn_experts_out': _L0_ffn_in['experts_out'], 'L1_xattn_W_q': _L1_xattn_in['W_q'], 'L1_xattn_b_q': _L1_xattn_in['b_q'], 'L1_xattn_W_k': _L1_xattn_in['W_k'], 'L1_xattn_b_k': _L1_xattn_in['b_k'], 'L1_xattn_W_v': _L1_xattn_in['W_v'], 'L1_xattn_b_v': _L1_xattn_in['b_v'], 'L1_xattn_W_o': _L1_xattn_in['W_o'], 'L1_xattn_b_o': _L1_xattn_in['b_o'], 'L1_ffn_w_router': _L1_ffn_in['w_router'], 'L1_ffn_W1': _L1_ffn_in['W1'], 'L1_ffn_b1': _L1_ffn_in['b1'], 'L1_ffn_W2': _L1_ffn_in['W2'], 'L1_ffn_b2': _L1_ffn_in['b2']}

def reference(x, ctx_1024, mask_Bx1x1xS2_ff0, L0_xattn_cq_w, L0_xattn_cq_b, L0_xattn_ck_w, L0_xattn_ck_b, L0_xattn_cv_w, L0_xattn_cv_b, L0_xattn_co_w, L0_xattn_co_b, L0_xattn_co_g, L0_xattn_co_be, L0_xattn_sq_w, L0_xattn_sq_b, L0_xattn_sk_w, L0_xattn_sk_b, L0_xattn_sv_w, L0_xattn_sv_b, L0_xattn_so_w, L0_xattn_so_b, L0_xattn_so_g, L0_xattn_so_be, L0_xattn_fi_w, L0_xattn_fi_b, L0_xattn_fo_w, L0_xattn_fo_b, L0_xattn_fo_g, L0_xattn_fo_be, L0_ffn_router_w, L0_ffn_router_b, L0_ffn_experts_inter, L0_ffn_experts_out, L1_xattn_W_q, L1_xattn_b_q, L1_xattn_W_k, L1_xattn_b_k, L1_xattn_W_v, L1_xattn_b_v, L1_xattn_W_o, L1_xattn_b_o, L1_ffn_w_router, L1_ffn_W1, L1_ffn_b1, L1_ffn_W2, L1_ffn_b2):
    import jax
    import jax.numpy as jnp

    def _L0_xattn_ref(input_tensor, ctx_tensor, ctx_attn_mask, cq_w, cq_b, ck_w, ck_b, cv_w, cv_b, co_w, co_b, co_g, co_be, sq_w, sq_b, sk_w, sk_b, sv_w, sv_b, so_w, so_b, so_g, so_be, fi_w, fi_b, fo_w, fo_b, fo_g, fo_be):
        import jax, jax.numpy as jnp
        import numpy as np
        H = 16
        D = 256
        F = 1024
        LN_EPS = 1e-05

        def _glorot(key, shape):
            fan_in, fan_out = (shape[0], shape[1])
            lim = np.sqrt(6.0 / (fan_in + fan_out))
            return jax.random.uniform(key, shape, jnp.float32, -lim, lim)

        def _split_heads(x):
            b, l, _ = x.shape
            return x.reshape(b, l, H, D // H)

        def _mha(x, ctx, mask, qw, qb, kw, kb, vw, vb):
            q = _split_heads(x @ qw + qb)
            k = _split_heads(ctx @ kw + kb)
            v = _split_heads(ctx @ vw + vb)
            scores = jnp.einsum('bqhd,bkhd->bhqk', q, k) / np.sqrt(D // H).astype(np.float32)
            if mask is not None:
                scores = scores + mask
            probs = jax.nn.softmax(scores, axis=-1)
            out = jnp.einsum('bhqk,bkhd->bqhd', probs, v)
            return out.reshape(x.shape[0], x.shape[1], D)

        def _self_output(h, residual, w, b, g, be):
            h = h @ w + b
            h = h + residual
            mu = jnp.mean(h, axis=-1, keepdims=True)
            var = jnp.mean(jnp.square(h - mu), axis=-1, keepdims=True)
            return (h - mu) * jax.lax.rsqrt(var + LN_EPS) * g + be
        ca = _mha(input_tensor, ctx_tensor, ctx_attn_mask, cq_w, cq_b, ck_w, ck_b, cv_w, cv_b)
        x = _self_output(ca, input_tensor, co_w, co_b, co_g, co_be)
        sa = _mha(x, x, None, sq_w, sq_b, sk_w, sk_b, sv_w, sv_b)
        x = _self_output(sa, x, so_w, so_b, so_g, so_be)
        inter = jax.nn.gelu(x @ fi_w + fi_b, approximate=False)
        x = _self_output(inter, x, fo_w, fo_b, fo_g, fo_be)
        return x

    def _L0_ffn_ref(x, router_w, router_b, experts_inter, experts_out):
        import math
        import jax, jax.numpy as jnp
        import numpy as np
        NUM_EXPERTS = 8
        TOP_K = 2
        CAPACITY_FACTOR = 1.0
        B, S, H, I = (4, 512, 256, 1024)
        batch, seq, hidden = x.shape
        n_exp = router_w.shape[0]
        n_tok = batch * seq
        cap = math.ceil(n_tok / n_exp * CAPACITY_FACTOR)
        logits = jnp.einsum('bsh,eh->bse', x, router_w) + router_b
        weights_flat = jax.nn.softmax(logits, axis=-1).reshape(n_tok, n_exp)
        x_flat = x.reshape(n_tok, hidden)
        topk_vals, topk_idx = jax.lax.top_k(weights_flat, TOP_K)
        rows = jnp.arange(n_tok)[:, None]
        topk_flat = jnp.zeros_like(weights_flat).at[rows, topk_idx].set(topk_vals)
        routing_mask = (topk_flat > 0).astype(jnp.int32)
        noop_w = topk_flat[:, -1]
        noop_mask = routing_mask[:, -1].astype(x.dtype)
        expert_w = topk_flat[:, :-1]
        expert_mask = routing_mask[:, :-1]
        sorted_indices = jnp.argsort(-expert_mask, axis=0)[:cap]
        sorted_mask = jnp.take_along_axis(expert_mask, sorted_indices, axis=0)
        used_idx = (sorted_indices * sorted_mask).reshape(-1)
        inputs = x_flat[used_idx] * sorted_mask.reshape(-1).astype(x.dtype)[:, None]
        inputs = inputs.reshape(cap, n_exp - 1, hidden)
        in_w = jnp.take_along_axis(expert_w, sorted_indices, axis=0)
        h = jax.nn.relu(jnp.einsum('ceh,ehi->cei', inputs, experts_inter))
        out = jnp.einsum('cei,eih->ceh', h, experts_out) * in_w[..., None]
        combined = jnp.zeros_like(x_flat).at[used_idx].add(out.reshape(-1, hidden))
        combined = combined + x_flat * (noop_w * noop_mask)[:, None]
        return combined.reshape(batch, seq, hidden)

    def _L1_xattn_ref(Q, K, V, W_q, b_q, W_k, b_k, W_v, b_v, W_o, b_o):
        import jax, jax.numpy as jnp
        import numpy as np
        D_MODEL = 256
        NUM_HEADS = 16
        D_K = D_MODEL // NUM_HEADS

        def _mha(Q, K, V, W_q, b_q, W_k, b_k, W_v, b_v, W_o, b_o):
            B, L, _ = Q.shape
            H, dk = (NUM_HEADS, D_K)
            q = (Q @ W_q.T + b_q).reshape(B, L, H, dk).transpose(0, 2, 1, 3)
            k = (K @ W_k.T + b_k).reshape(B, L, H, dk).transpose(0, 2, 1, 3)
            v = (V @ W_v.T + b_v).reshape(B, L, H, dk).transpose(0, 2, 1, 3)
            scale = jnp.sqrt(jnp.float32(dk))
            scores = jnp.einsum('bhqd,bhkd->bhqk', q, k) / scale
            attn = jax.nn.softmax(scores, axis=-1)
            out = jnp.einsum('bhqk,bhkd->bhqd', attn, v)
            out = out.transpose(0, 2, 1, 3).reshape(B, L, H * dk)
            return out @ W_o.T + b_o
        return _mha(Q, K, V, W_q, b_q, W_k, b_k, W_v, b_v, W_o, b_o)

    def _L1_ffn_ref(hidden_states, w_router, W1, b1, W2, b2):
        import jax, jax.numpy as jnp
        import numpy as np
        CAPACITY_FACTOR = 0.5
        'Mixture-of-Depths block: route top-k tokens through an FFN inner block,\n            scatter back with sigmoid router weights; bypassed tokens pass through.'
        B, S, D = hidden_states.shape
        k = int(S * CAPACITY_FACTOR)
        scores = jnp.einsum('bsd,d->bs', hidden_states, w_router)
        top_scores, top_idx = jax.lax.top_k(scores, k)
        weights = jax.nn.sigmoid(top_scores)
        selected = jnp.take_along_axis(hidden_states, top_idx[:, :, None], axis=1)
        h = jax.nn.gelu(jnp.einsum('bkd,df->bkf', selected, W1) + b1)
        processed = jnp.einsum('bkf,fd->bkd', h, W2) + b2
        update = weights[:, :, None] * processed

        def scatter_one(xb, ib, ub):
            return xb.at[ib].add(ub)
        output = jax.vmap(scatter_one)(hidden_states, top_idx, update)
        return output
    x = x + _L0_xattn_ref(_layernorm(x, axis=-1), ctx_1024, mask_Bx1x1xS2_ff0, L0_xattn_cq_w, L0_xattn_cq_b, L0_xattn_ck_w, L0_xattn_ck_b, L0_xattn_cv_w, L0_xattn_cv_b, L0_xattn_co_w, L0_xattn_co_b, L0_xattn_co_g, L0_xattn_co_be, L0_xattn_sq_w, L0_xattn_sq_b, L0_xattn_sk_w, L0_xattn_sk_b, L0_xattn_sv_w, L0_xattn_sv_b, L0_xattn_so_w, L0_xattn_so_b, L0_xattn_so_g, L0_xattn_so_be, L0_xattn_fi_w, L0_xattn_fi_b, L0_xattn_fo_w, L0_xattn_fo_b, L0_xattn_fo_g, L0_xattn_fo_be)
    x = x + _L0_ffn_ref(_layernorm(x, axis=-1), L0_ffn_router_w, L0_ffn_router_b, L0_ffn_experts_inter, L0_ffn_experts_out)
    x = x + _L1_xattn_ref(_layernorm(x, axis=-1), ctx_1024, ctx_1024, L1_xattn_W_q, L1_xattn_b_q, L1_xattn_W_k, L1_xattn_b_k, L1_xattn_W_v, L1_xattn_b_v, L1_xattn_W_o, L1_xattn_b_o)
    x = x + _L1_ffn_ref(_layernorm(x, axis=-1), L1_ffn_w_router, L1_ffn_W1, L1_ffn_b1, L1_ffn_W2, L1_ffn_b2)
    return x

_drawn_inputs = setup_inputs


def setup_inputs(seed=0):
    import zlib

    import numpy as np

    out = dict(_drawn_inputs(seed))
    spreads = {'L0_xattn_cq_b': (0.0, 0.402),
     'L0_xattn_ck_b': (0.0, 0.8),
     'L0_xattn_cv_b': (0.0, 0.1),
     'L0_xattn_co_b': (0.0, 0.1),
     'L0_xattn_co_g': (1.0, 0.2),
     'L0_xattn_co_be': (0.0, 0.1),
     'L0_xattn_sq_b': (0.0, 0.77),
     'L0_xattn_sk_b': (0.0, 0.8),
     'L0_xattn_sv_b': (0.0, 0.1),
     'L0_xattn_so_b': (0.0, 0.1),
     'L0_xattn_so_g': (1.0, 0.2),
     'L0_xattn_so_be': (0.0, 0.1),
     'L0_xattn_fi_b': (0.0, 0.1),
     'L0_xattn_fo_b': (0.0, 0.1),
     'L0_xattn_fo_g': (1.0, 0.2),
     'L0_xattn_fo_be': (0.0, 0.1),
     'L0_ffn_router_b': (0.0, 0.1),
     'L1_ffn_b1': (0.0, 0.75),
     'L1_ffn_b2': (0.0, 0.5)}
    factors = {'L1_xattn_b_q': 6.313, 'L1_xattn_b_k': 8.0}
    for name, (base, spread) in spreads.items():
        noise = np.random.default_rng([zlib.crc32(name.encode()), seed]).standard_normal(out[name].shape)
        drawn = base * np.exp(spread * noise) if base else spread * noise
        out[name] = jnp.asarray(drawn.astype(out[name].dtype))
    for name, factor in factors.items():
        out[name] = (out[name] * factor).astype(out[name].dtype)
    return out
```

```python
from contextlib import ExitStack

import concourse.bass as bass
import numpy as np
from concourse import mybir

F32 = mybir.dt.float32
F32R = mybir.dt.float32r
U32 = mybir.dt.uint32
ACT = mybir.ActivationFunctionType
ALU = mybir.AluOpType
AX = mybir.AxisListType

P = 128
B, S, D, H = 8, 256, 256, 16
DH = D // H
NT = B * S // P
TB = S // P
KD = D // P
HG = H // 2
F = 1024
KF = F // P
NE = 7
CAP = B * S // 8
K_SELECT = S // 2
EPS = 1e-5
MASK_ROW = 3 * DH
MAX_ROW = MASK_ROW + 2
SROWS = MASK_ROW + 2
STROWS = MAX_ROW + 1
NBANK = 4
NPT = 8

(R_CV, R_CO, R_CG, R_CBE, R_SV, R_SO, R_SG, R_SBE, R_FO, R_FG, R_FBE) = range(11)
(R_LV, R_LO, R_B2, R_RT) = range(4)


class Chain:

    def __init__(self, eng, sem):
        self.eng, self.sem, self.n = eng, sem, 0

    def __call__(self, ins):
        self.n += 1
        ins.then_inc(self.sem, 1)
        self.eng.wait_ge(self.sem, self.n)


def build(nc, x, ctxT, mask, wA, colA, rowA, fi, fo, fib, rw, rb, ein, eout, wC, colC, rowC, w1, w2, b1, out):
    moe_in = nc.dram_tensor("moe_in", [NE * CAP, D], F32, kind="Internal").ap()
    moe_out = nc.dram_tensor("moe_out", [NE * CAP + 1, D], F32, kind="Internal").ap()
    x_t = x.rearrange("(t p) d -> p t d", p=P)
    out_t = out.rearrange("(t p) d -> p t d", p=P)

    root = ExitStack()
    scope = [root]

    def sb(name, shape, dt=F32):
        return scope[-1].enter_context(nc.sbuf_tensor(name, shape, dt))

    def sem(name):
        return root.enter_context(nc.semaphore(name))

    with root:
        sc = [root.enter_context(nc.psum_tensor(f"score{i}", [P, 512], F32)) for i in range(NBANK)]
        dn = [root.enter_context(nc.psum_tensor(f"dense{i}", [P, 512], F32)) for i in range(3)]
        po = root.enter_context(nc.psum_tensor("pv_out", [P, 512], F32))

        xres = sb("xres", [P, NT, D])
        ident = sb("ident", [P, P])
        half = sb("half", [P, 2])
        qstack = sb("qstack", [P, HG, S], F32R)
        kstack = [sb("kstack_cross", [P, HG, S], F32R), sb("kstack_plain", [P, HG, S], F32R)]
        vext = sb("vext", [P, TB, H, 2 * DH])
        ctx_raw = sb("ctx_raw", [P, KD, S])
        c_hi = sb("c_hi", [P, KD, S], F32R)
        c_lo = sb("c_lo", [P, KD, S], F32R)
        hT_hi = sb("hT_hi", [P, KD, S], F32R)
        hT_lo = sb("hT_lo", [P, KD, S], F32R)
        q32 = sb("q32", [P, 2, S])
        q_hi = sb("q_hi", [P, 2, S], F32R)
        q_lo = sb("q_lo", [P, 2, S], F32R)
        k32 = sb("k32", [P, 2, S])
        k_hi = sb("k_hi", [P, 2, S], F32R)
        k_lo = sb("k_lo", [P, 2, S], F32R)
        nmax = sb("nmax", [P, 2, TB, HG])
        m_hi = sb("m_hi", [HG, 2, S], F32R)
        probs = sb("probs", [P, NPT, TB, S])
        oext = sb("oext", [P, 4, S])
        rsum = sb("rsum", [P, TB, H])
        h = sb("h", [P, TB, D])
        res = sb("res", [P, TB, D])
        resb = sb("resb", [P, TB, D])
        norm = sb("norm", [P, TB, D])
        attn = norm
        bn = sb("bn", [P, TB, 6])
        mv = sb("mv", [P, TB, 2])
        var = sb("var", [P, TB])
        rstd = sb("rstd", [P, TB])

        names = """ld wsplit setup mask_ld mask_rows stk_mask ctx_ld ctx_hi ctx_split h_ready hT_ps hT_hi_s hT_ready
            k_ps q_ps v_ps k32_s q32_s k_split q_split v_ready stk_k stk_q s_ps s_max mT_ps m_row stk_m0 stk_m1
            st_ps exp_done pv_ps o_ev oT_ps o_norm o2_ps o2_hi o2_ready op_ps resb_ready ln_var ln_rstd
            chain pchain fc1_ps gelu hid_hi hid_ready fc2_ps xn_ready log_ps st_x raw_free route_e route_m
            cum_ps route_i wload0 wload1 scat w_free y_ready x_ld srow_ps onehot sel_ps selT_hi selT_ready ohT_ps ohT_ready
            proc_ready upd_ps x_out st_out sig_e""".split() + [f"gath{t}" for t in range(NT)]
        sm = {n: sem(n) for n in names}

        def clear():
            for n in names:
                nc.gpsimd.sem_clear(sm[n])
            nc.all_engine_barrier()

        def mm3(pe, dst, lhs, rhs, first, last):
            pe.matmul(dst, lhs[0], rhs[0], start=first, stop=False)
            pe.matmul(dst, lhs[1], rhs[0], start=False, stop=False)
            return pe.matmul(dst, lhs[0], rhs[1], start=False, stop=last)

        def pe_project_T(pe, dst, w, src):
            for m in range(KD):
                for k in range(KD):
                    last = mm3(pe, dst[:, m * S:(m + 1) * S],
                               [v[:, k, m * P:(m + 1) * P] for v in w], [v[:, k, :] for v in src], k == 0, k == KD - 1)
            return last

        def pe_project(pe, dst, w, src):
            for t in range(TB):
                for k in range(KD):
                    last = mm3(pe, dst[:, t * D:(t + 1) * D],
                               [v[:, k, t * P:(t + 1) * P] for v in src], [v[:, k, :] for v in w], k == 0, k == KD - 1)
            return last

        def pe_transpose(pe, dst, src):
            for k in range(KD):
                for t in range(TB):
                    last = pe.transpose(dst[:, k * S + t * P:k * S + (t + 1) * P], src[:, t, k * P:(k + 1) * P], ident[:])
            return last

        def pe_h_T(pe, n):
            pe.wait_ge(sm["h_ready"], n + 1)
            pe_transpose(pe, dn[0], h).then_inc(sm["hT_ps"], 1)

        def act_h_T(act, n):
            act.wait_ge(sm["hT_ps"], n + 1)
            act.activation(hT_hi[:].rearrange("p k s -> p (k s)"), dn[0][:, :], ACT.Copy).then_inc(sm["hT_hi_s"], 1)

        def dve_h_T(dve, n):
            dve.wait_ge(sm["hT_hi_s"], n + 1)
            dve.tensor_tensor(hT_lo[:].rearrange("p k s -> p (k s)"), dn[0][:, :],
                              hT_hi[:].rearrange("p k s -> p (k s)").bitcast(F32), ALU.subtract).then_inc(sm["hT_ready"], 1)

        def pe_attention(pe, a, n_h, kst, nxt):
            pe.wait_ge(sm["stk_k"], 96 * (a + 1))
            pe.wait_ge(sm["stk_q"], 96 * (a + 1))

            def first(i):
                g, s = i // 2, i % 2
                if i >= NBANK:
                    pe.wait_ge(sm["s_max"], H * a + i - NBANK + 1)
                for t in range(TB):
                    last = pe.matmul(sc[i % NBANK][:, t * S:(t + 1) * S], qstack[64 * s:64 * s + SROWS, g, t * P:(t + 1) * P],
                                     kst[64 * s:64 * s + SROWS, g, :], start=True, stop=True)
                last.then_inc(sm["s_ps"], 1)

            def max_T(j):
                pe.wait_ge(sm["s_max"], H * a + HG * (j + 1))
                if j == 0:
                    pe.wait_ge(sm["k32_s"], a + 1)
                else:
                    pe.wait_ge(sm["v_ready"], a + 1)
                for t in range(TB):
                    last = pe.transpose(dn[1 + j][0:HG, t * P:(t + 1) * P], nmax[:, j, t, :], ident[:])
                last.then_inc(sm["mT_ps"], 1)

            def second(i):
                g, s = i // 2, i % 2
                if i < NBANK:
                    pe.wait_ge(sm["s_max"], H * a + H - NBANK + i + 1)
                else:
                    pe.wait_ge(sm["exp_done"], H * a + i - NBANK + 1)
                if i % HG == 0:
                    pe.wait_ge(sm[f"stk_m{i // HG}"], 32 * (a + 1))
                for t in range(TB):
                    last = pe.matmul(sc[i % NBANK][:, t * S:(t + 1) * S], kst[64 * s:64 * s + STROWS, g, t * P:(t + 1) * P],
                                     qstack[64 * s:64 * s + STROWS, g, :], start=True, stop=True)
                last.then_inc(sm["st_ps"], 1)

            def pv(u):
                pe.wait_ge(sm["exp_done"], H * a + 4 * u + 4)
                pe.wait_ge(sm["v_ready"], a + 1)
                if u >= 2:
                    pe.wait_ge(sm["o_ev"], 4 * a + u - 1)
                for t in range(TB):
                    for j in range(4):
                        i = 4 * u + j
                        head = (i % 2) * HG + i // 2
                        last = pe.matmul((po, dn[1])[u % 2][32 * j:32 * j + 32, 0:S], vext[:, t, head, :],
                                         probs[:, i % NPT, t, :], start=(t == 0), stop=(t == TB - 1),
                                         tile_position=(0, 32 * j), skip_group_check=True)
                last.then_inc(sm["pv_ps"], 1)

            for i in range(12):
                first(i)
            max_T(0)
            for i in range(12, H):
                first(i)
            max_T(1)
            for u in range(4):
                for i in range(4 * u, 4 * u + 4):
                    second(i)
                if u >= 1:
                    pv(u - 1)
            pv(3)
            pe.wait_ge(sm["o_ev"], 4 * a + 4)
            for t in range(TB):
                for u in range(4):
                    last = pe.transpose(dn[t][:, u * P:(u + 1) * P], oext[:, u, t * P:(t + 1) * P], ident[:])
                last.then_inc(sm["oT_ps"], 1)
            pe.wait_ge(sm["o_norm"], a + 1)
            pe_transpose(pe, dn[2], attn).then_inc(sm["o2_ps"], 1)
            pe.wait_ge(sm["o2_ready"], a + 1)
            pe_project(pe, dn[0], nxt, (hT_hi, hT_lo)).then_inc(sm["op_ps"], 1)

        def act_qk(act, a, which, bank, col):
            dst, scale = (q32, 1.0 / np.sqrt(DH)) if which == "q" else (k32, 1.0)
            act.wait_ge(sm[f"{which}_ps"], a + 1)
            for m in range(KD):
                last = act.activation(dst[:, m, :], bank[:, m * S:(m + 1) * S], ACT.Identity, bias=col[:, m:m + 1], scale=float(scale))
            last.then_inc(sm[f"{which}32_s"], 1)

        def act_attention(act, a):
            for i in range(H):
                act.wait_ge(sm["st_ps"], H * a + i + 1)
                if i >= NPT:
                    act.wait_ge(sm["pv_ps"], 4 * a + (i - NPT) // 4 + 1)
                act.activation(probs[:, i % NPT, :, :].rearrange("p t s -> p (t s)"), sc[i % NBANK][:, :], ACT.Exp).then_inc(sm["exp_done"], 1)
            act.wait_ge(sm["o2_ps"], a + 1)
            act.activation(hT_hi[:].rearrange("p k s -> p (k s)"), dn[2][:, :], ACT.Copy).then_inc(sm["o2_hi"], 1)

        def dve_qkv(dve, ch, a, vrow):
            for which, full, hi, lo in (("q", q32, q_hi, q_lo), ("k", k32, k_hi, k_lo)):
                dve.wait_ge(sm[f"{which}32_s"], a + 1)
                ch(dve.tensor_copy(hi[:], full[:]))
                dve.tensor_tensor(lo[:], full[:], hi[:].bitcast(F32), ALU.subtract).then_inc(sm[f"{which}_split"], 1)
            dve.wait_ge(sm["v_ps"], a + 1)
            for t in range(TB):
                last = dve.tensor_tensor(vext[:, t, :, 0:DH], dn[2][:, t * D:(t + 1) * D].rearrange("p (h d) -> p h d", d=DH),
                                         vrow.rearrange("p (h d) -> p h d", d=DH), ALU.add)
            last.then_inc(sm["v_ready"], 1)

        def dve_attention(dve, ch, a):
            def row_max(i):
                j, slot = i // HG, (i % 2) * (HG // 2) + (i % HG) // 2
                dve.wait_ge(sm["s_ps"], H * a + i + 1)
                dve.tensor_reduce(nmax[:, j, :, slot], sc[i % NBANK][:, :].rearrange("p (t s) -> p t s", t=TB), AX.X, ALU.max,
                                  negate=True).then_inc(sm["s_max"], 1)

            def max_row(j):
                dve.wait_ge(sm["mT_ps"], 2 * a + j + 1)
                dve.tensor_copy(m_hi[:, j, :], dn[1 + j][0:HG, 0:S]).then_inc(sm["m_row"], 1)

            for i in range(12):
                row_max(i)
            max_row(0)
            for i in range(12, H):
                row_max(i)
            max_row(1)
            for u in range(4):
                dve.wait_ge(sm["pv_ps"], 4 * a + u + 1)
                dve.tensor_copy(oext[:, u, :], (po, dn[1])[u % 2][:, 0:S]).then_inc(sm["o_ev"], 1)
            for t in range(TB):
                dve.wait_ge(sm["oT_ps"], 2 * a + t + 1)
                grp = dn[t][:, :].rearrange("p (g s e) -> p g s e", s=2, e=2 * DH)
                ch(dve.reciprocal(rsum[:, t, :].rearrange("p (g s) -> p g s", s=2), grp[:, :, :, DH]))
                last = dve.tensor_tensor(attn[:, t, :].rearrange("p (s g d) -> p g s d", s=2, g=HG), grp[:, :, :, 0:DH],
                                         rsum[:, t, :].rearrange("p (g s) -> p g s", s=2).unsqueeze(3).to_broadcast([P, HG, 2, DH]), ALU.mult)
            last.then_inc(sm["o_norm"], 1)
            dve.wait_ge(sm["o2_hi"], a + 1)
            dve.tensor_tensor(hT_lo[:].rearrange("p k s -> p (k s)"), dn[2][:, :],
                              hT_hi[:].rearrange("p k s -> p (k s)").bitcast(F32), ALU.subtract).then_inc(sm["o2_ready"], 1)

        def dve_norm(dve, ch, n, src):
            for t in range(TB):
                last = dve.bn_stats(bn[:, t, :], src[:, t, :])
            ch(last)
            for t in range(TB):
                last = dve.bn_aggr(mv[:, t, :], bn[:, t, :])
            ch(last)
            dve.tensor_scalar(var[:, :], mv[:, :, 1], EPS, None, ALU.add).then_inc(sm["ln_var"], 1)
            dve.wait_ge(sm["ln_rstd"], n + 1)

        def dve_norm_apply(dve, src, dst):
            for t in range(TB):
                last = dve.tensor_scalar(dst[:, t, :], src[:, t, :], mv[:, t, 0:1], rstd[:, t:t + 1], ALU.subtract, ALU.mult)
            return last

        def dve_affine(dve, ch, g, be, dst):
            ch(dve.tensor_tensor(norm[:], norm[:], g.unsqueeze(1).to_broadcast([P, TB, D]), ALU.mult))
            return dve.tensor_tensor(dst, norm[:], be, ALU.add)

        def pool_rstd(gp, n):
            gp.wait_ge(sm["ln_var"], n + 1)
            gp.tensor_tensor(rstd[:, :], var[:, :], half[:, :], ALU.pow).then_inc(sm["ln_rstd"], 1)

        def sp_stack(sp, which):
            parts, dst = ((q_hi, q_hi, q_lo), qstack) if which == "q" else ((k_hi, k_lo, k_hi), None)
            return parts, dst

        def sp_stack_all(sp, a, which, dst):
            parts, _ = sp_stack(sp, which)
            sp.wait_ge(sm[f"{which}_split"], a + 1)
            for s in range(2):
                for c in range(3):
                    sp.dma_start(dst[64 * s + DH * c:64 * s + DH * (c + 1), :, :].bitcast(F32), parts[c][:, s, :].bitcast(F32)).then_inc(sm[f"stk_{which}"], 16)

        def sp_stack_max(sp, a, queue=None):
            for j in range(2):
                sp.wait_ge(sm["m_row"], 2 * a + j + 1)
                for s in range(2):
                    sp.dma_start(qstack[64 * s + MAX_ROW:64 * s + MAX_ROW + 1, 4 * j:4 * j + 4, :].bitcast(F32),
                                 m_hi[4 * s:4 * s + 4, j, :].bitcast(F32)).then_inc(sm[f"stk_m{j}"], 16)

        def load_split(weights):
            stage = [probs[:, 4 * i:4 * i + 4, :, :].rearrange("p a t s -> p (a t s)") for i in range(2)]
            if True:
                with nc.Block() as block:
                    @block.sync
                    def _(sp):
                        for i, (src, hi, lo) in enumerate(weights):
                            if i >= 2:
                                sp.wait_ge(sm["raw_free"], i - 1)
                            n = src.shape[1] * src.shape[2]
                            sp.dma_start(stage[i % 2][:, 0:n].rearrange("p (a b) -> p a b", a=src.shape[1]), src).then_inc(sm[f"wload{i % 2}"], 16)

                    @block.vector
                    def _(dve):
                        for i, (src, hi, lo) in enumerate(weights):
                            n = src.shape[1] * src.shape[2]
                            raw = stage[i % 2][:, 0:n].rearrange("p (a b) -> p a b", a=src.shape[1])
                            dve.wait_ge(sm[f"wload{i % 2}"], 16 * (i // 2 + 1))
                            dve.tensor_copy(hi, raw).then_inc(sm["w_free"], 1)
                            dve.wait_ge(sm["w_free"], i + 1)
                            dve.tensor_tensor(lo, raw, hi.bitcast(F32), ALU.subtract).then_inc(sm["raw_free"], 1)
                clear()

        with ExitStack() as st0:
            zeros = st0.enter_context(nc.sbuf_tensor("zeros", [P, NE * CAP // P, D], F32))
            zero2k = st0.enter_context(nc.sbuf_tensor("zero2k", [1, 2, HG * S], F32R))
            with nc.Block() as block:
                @block.sync
                def _(sp):
                    sp.dma_start(xres[:], x_t).then_inc(sm["ld"], 16)
                    sp.wait_ge(sm["setup"], 5)
                    sp.dma_start(moe_in.rearrange("(t p) d -> p t d", p=P), zeros[:]).then_inc(sm["ld"], 16)
                    sp.dma_start(moe_out[NE * CAP:NE * CAP + 1, :], zeros[0:1, 0, :]).then_inc(sm["ld"], 16)
                    for s in range(2):
                        sp.dma_start(kstack[1][64 * s + MASK_ROW:64 * s + MASK_ROW + 2, :, :].bitcast(F32), zero2k[:].bitcast(F32)).then_inc(sm["ld"], 16)
                    sp.wait_ge(sm["ld"], 80)

                @block.gpsimd
                def _(gp):
                    gp.memset(ident[:], 0.0).then_inc(sm["pchain"], 1)
                    gp.memset(half[:], -0.5)
                    gp.wait_ge(sm["pchain"], 1)
                    gp.affine_select(out=ident[:], in_=ident[:], compare_op=ALU.not_equal, fill=1.0, base=0,
                                     pattern=[[-1, P]], channel_multiplier=1)
                    gp.memset(vext[:], 1.0)

                @block.vector
                def _(dve):
                    dve.memset(zeros[:], 0.0).then_inc(sm["setup"], 1)
                    dve.memset(zero2k[:].bitcast(F32), 0.0).then_inc(sm["setup"], 1)
                    for t in (qstack, kstack[0], kstack[1]):
                        dve.memset(t[:].bitcast(F32), 1.0).then_inc(sm["setup"], 1)
            clear()

        xn = sb("xn", [P, NT, D])
        lg = sb("lg", [P, NT, 8])

        with ExitStack() as stA:
            scope.append(stA)
            wq = [(sb(f"wA_hi{i}", [P, KD, D], F32R), sb(f"wA_lo{i}", [P, KD, D], F32R)) for i in range(8)]
            fiw = (sb("fi_hi", [P, KD, F], F32R), sb("fi_lo", [P, KD, F], F32R))
            fow = (sb("fo_hi", [P, KF, D], F32R), sb("fo_lo", [P, KF, D], F32R))
            rww = (sb("rw_hi", [P, KD, 8], F32R), sb("rw_lo", [P, KD, 8], F32R))
            load_split([(wA[i].rearrange("(k p) n -> p k n", p=P), wq[i][0][:], wq[i][1][:]) for i in range(8)]
                       + [(fi.rearrange("(k p) n -> p k n", p=P), fiw[0][:], fiw[1][:]),
                          (fo.rearrange("(k p) n -> p k n", p=P), fow[0][:], fow[1][:]),
                          (rw.rearrange("(k p) n -> p k n", p=P), rww[0][:], rww[1][:])])
            rows = sb("rowsA", [P, 11, D])
            cols = sb("colsA", [P, 4, KD])
            fibc = sb("fib", [P, KF])
            rbr = sb("rbr", [P, 8])
            mrow = q32[0:1, 0, :]
            mhl = m_hi[0:1, :, :]
            g32 = probs[:, 0:4, :, :].rearrange("p a t s -> p (a t) s")
            g_hi = sb("g_hi", [P, KF, S], F32R)
            g_lo = sb("g_lo", [P, KF, S], F32R)
            CQ, CK, CV, CO, SQ, SK, SV, SO = wq

            with nc.Block() as block:
                @block.sync
                def _(sp):
                    sp.dma_start(rows[:], rowA.unsqueeze(0).to_broadcast([P, 11, D])).then_inc(sm["ld"], 16)
                    sp.dma_start(cols[:], colA).then_inc(sm["ld"], 16)
                    sp.dma_start(fibc[:], fib).then_inc(sm["ld"], 16)
                    sp.dma_start(rbr[:], rb.to_broadcast([P, 8])).then_inc(sm["ld"], 16)

                @block.vector
                def _(dve):
                    dve.wait_ge(sm["ld"], 64)
                    for i in (0, 2):
                        dve.tensor_scalar(cols[:, i, :], cols[:, i, :], float(1.0 / np.sqrt(DH)), None, ALU.mult).then_inc(sm["setup"], 1)
                    dve.wait_ge(sm["setup"], 2)
            clear()

            with nc.Fori(0, B) as b:
                with nc.Block() as block:
                    xb = xres[:, bass.ts(b, TB), :]

                    @block.sync
                    def _(sp):
                        sp.dma_start(ctx_raw[:], ctxT[bass.ts(b, 1), :, :].rearrange("o (k p) s -> p (o k) s", p=P)).then_inc(sm["ctx_ld"], 16)
                        sp.dma_start(mrow, mask[bass.ts(b, 1), :]).then_inc(sm["mask_ld"], 16)
                        sp_stack_all(sp, 0, "k", kstack[0])
                        sp.wait_ge(sm["mask_rows"], 2)
                        for s in range(2):
                            for c, part in enumerate((g_hi, g_lo)):
                                sp.dma_start(kstack[0][64 * s + MASK_ROW + c:64 * s + MASK_ROW + c + 1, :, :].bitcast(F32), part[0:1, :, :].bitcast(F32)).then_inc(sm["stk_mask"], 16)
                        sp_stack_all(sp, 0, "q", qstack)
                        sp_stack_max(sp, 0)
                        sp_stack_all(sp, 1, "q", qstack)
                        sp_stack_all(sp, 1, "k", kstack[1])
                        sp_stack_max(sp, 1)

                    @block.tensor
                    def _(pe):
                        pe.wait_ge(sm["ctx_split"], 1)
                        pe_project_T(pe, dn[1], CK, (c_hi, c_lo)).then_inc(sm["k_ps"], 1)
                        pe_project(pe, dn[2], CV, (c_hi, c_lo)).then_inc(sm["v_ps"], 1)
                        pe_h_T(pe, 0)
                        pe.wait_ge(sm["hT_ready"], 1)
                        pe_project_T(pe, dn[0], CQ, (hT_hi, hT_lo)).then_inc(sm["q_ps"], 1)
                        pe.wait_ge(sm["stk_mask"], 64)
                        pe_attention(pe, 0, 0, kstack[0], CO)
                        pe_h_T(pe, 1)
                        pe.wait_ge(sm["hT_ready"], 2)
                        pe_project_T(pe, dn[1], SK, (hT_hi, hT_lo)).then_inc(sm["k_ps"], 1)
                        pe_project_T(pe, dn[0], SQ, (hT_hi, hT_lo)).then_inc(sm["q_ps"], 1)
                        pe_project(pe, dn[2], SV, (hT_hi, hT_lo)).then_inc(sm["v_ps"], 1)
                        pe_attention(pe, 1, 1, kstack[1], SO)
                        pe_h_T(pe, 2)
                        pe.wait_ge(sm["hT_ready"], 3)
                        for j, bank in enumerate((dn[1], dn[2], po, sc[0])):
                            for m in (2 * j, 2 * j + 1):
                                for k in range(KD):
                                    last = mm3(pe, bank[:, (m % 2) * S:(m % 2 + 1) * S], [v[:, k, m * P:(m + 1) * P] for v in fiw],
                                               [hT_hi[:, k, :], hT_lo[:, k, :]], k == 0, k == KD - 1)
                            last.then_inc(sm["fc1_ps"], 1)
                        for t in range(TB):
                            for k in range(KF):
                                if t == 0:
                                    pe.wait_ge(sm["hid_ready"], k + 1)
                                last = mm3(pe, sc[1][:, t * D:(t + 1) * D], [g_hi[:, k, t * P:(t + 1) * P], g_lo[:, k, t * P:(t + 1) * P]],
                                           [fow[0][:, k, :], fow[1][:, k, :]], k == 0, k == KF - 1)
                        last.then_inc(sm["fc2_ps"], 1)
                        pe_h_T(pe, 3)
                        pe.wait_ge(sm["hT_ready"], 4)
                        for t in range(TB):
                            for k in range(KD):
                                last = mm3(pe, dn[1][:, t * 8:(t + 1) * 8], [hT_hi[:, k, t * P:(t + 1) * P], hT_lo[:, k, t * P:(t + 1) * P]],
                                           [rww[0][:, k, :], rww[1][:, k, :]], k == 0, k == KD - 1)
                        last.then_inc(sm["log_ps"], 1)

                    @block.scalar
                    def _(act):
                        act.wait_ge(sm["ctx_ld"], 16)
                        act.activation(c_hi[:], ctx_raw[:], ACT.Copy).then_inc(sm["ctx_hi"], 1)
                        act_qk(act, 0, "k", dn[1], cols[:, 1, :])
                        act_h_T(act, 0)
                        act_qk(act, 0, "q", dn[0], cols[:, 0, :])
                        act_attention(act, 0)
                        act_h_T(act, 1)
                        act_qk(act, 1, "k", dn[1], cols[:, 3, :])
                        act_qk(act, 1, "q", dn[0], cols[:, 2, :])
                        act_attention(act, 1)
                        act_h_T(act, 2)
                        for m in range(KF):
                            act.wait_ge(sm["fc1_ps"], m // 2 + 1)
                            act.activation(g32[:, m, :], (dn[1], dn[2], po, sc[0])[m // 2][:, (m % 2) * S:(m % 2 + 1) * S], ACT.Gelu,
                                           bias=fibc[:, m:m + 1]).then_inc(sm["gelu"], 1)
                        act_h_T(act, 3)

                    @block.gpsimd
                    def _(gp):
                        pool_rstd(gp, 0)
                        gp.wait_ge(sm["chain"], 1)
                        for c, part in enumerate((g_hi, g_lo)):
                            gp.tensor_copy(part[0:1, :, :], mhl[:, c, :].unsqueeze(1).to_broadcast([1, HG, S])).then_inc(sm["mask_rows"], 1)
                        for n, row in enumerate((R_CO, R_SO, R_FO)):
                            gp.wait_ge(sm["h_ready"], n + 1)
                            if n == 2:
                                for m in range(KF):
                                    gp.wait_ge(sm["gelu"], m + 1)
                                    gp.tensor_copy(g_hi[:, m, :], g32[:, m, :]).then_inc(sm["hid_hi"], 1)
                            gp.tensor_tensor(resb[:], h[:], rows[:, row, :].unsqueeze(1).to_broadcast([P, TB, D]), ALU.add).then_inc(sm["resb_ready"], 1)
                            pool_rstd(gp, n + 1)
                        pool_rstd(gp, 4)

                    @block.vector
                    def _(dve):
                        ch = Chain(dve, sm["chain"])
                        dve.wait_ge(sm["mask_ld"], 16)
                        dve.tensor_copy(mhl[:, 0, :], mrow).then_inc(sm["setup"], 1)
                        dve.wait_ge(sm["setup"], 1)
                        ch(dve.tensor_tensor(mhl[:, 1, :], mrow, mhl[:, 0, :].bitcast(F32), ALU.subtract))
                        dve_norm(dve, ch, 0, xb)
                        dve_norm_apply(dve, xb, h).then_inc(sm["h_ready"], 1)
                        dve.wait_ge(sm["ctx_hi"], 1)
                        dve.tensor_tensor(c_lo[:], ctx_raw[:], c_hi[:].bitcast(F32), ALU.subtract).then_inc(sm["ctx_split"], 1)
                        dve_h_T(dve, 0)
                        for a, (row, g, be) in enumerate(((R_CV, R_CG, R_CBE), (R_SV, R_SG, R_SBE))):
                            dve_qkv(dve, ch, a, rows[:, row, :])
                            dve_attention(dve, ch, a)
                            dve.wait_ge(sm["op_ps"], a + 1)
                            dve.wait_ge(sm["resb_ready"], a + 1)
                            ch(dve.tensor_tensor(res[:].rearrange("p t d -> p (t d)"), dn[0][:, :], resb[:].rearrange("p t d -> p (t d)"), ALU.add))
                            dve_norm(dve, ch, a + 1, res)
                            ch(dve_norm_apply(dve, res, norm))
                            dve_affine(dve, ch, rows[:, g, :], rows[:, be, :].unsqueeze(1).to_broadcast([P, TB, D]), h[:]).then_inc(sm["h_ready"], 1)
                            dve_h_T(dve, a + 1)
                        for m in range(KF):
                            dve.wait_ge(sm["hid_hi"], m + 1)
                            dve.tensor_tensor(g_lo[:, m, :], g32[:, m, :], g_hi[:, m, :].bitcast(F32), ALU.subtract).then_inc(sm["hid_ready"], 1)
                        dve.wait_ge(sm["fc2_ps"], 1)
                        dve.wait_ge(sm["resb_ready"], 3)
                        ch(dve.tensor_tensor(res[:].rearrange("p t d -> p (t d)"), sc[1][:, :], resb[:].rearrange("p t d -> p (t d)"), ALU.add))
                        dve_norm(dve, ch, 3, res)
                        ch(dve_norm_apply(dve, res, norm))
                        ch(dve_affine(dve, ch, rows[:, R_FG, :], rows[:, R_FBE, :].unsqueeze(1).to_broadcast([P, TB, D]), norm[:]))
                        ch(dve.tensor_tensor(xb, xb, norm[:], ALU.add))
                        dve_norm(dve, ch, 4, xb)
                        ch(dve_norm_apply(dve, xb, h))
                        dve.tensor_copy(xn[:, bass.ts(b, TB), :], h[:]).then_inc(sm["h_ready"], 1)
                        dve_h_T(dve, 3)
                        dve.wait_ge(sm["log_ps"], 1)
                        ch(dve.tensor_tensor(lg[:, bass.ts(b, TB), :], dn[1][:, 0:16].rearrange("p (t e) -> p t e", e=8),
                                             rbr[:].unsqueeze(1).to_broadcast([P, TB, 8]), ALU.add))
                clear()
            scope.pop()

        with ExitStack() as stB:
            scope.append(stB)
            sh = [P, NT, 8]
            wts = sb("wts", sh)
            rank = sb("rank", sh)
            tmp = sb("tmp", sh)
            rmask = sb("rmask", sh)
            slot = sb("slot", sh)
            valid = sb("valid", sh)
            off = sb("off", sh)
            ebase = sb("ebase", sh)
            red = sb("red", [P, NT])
            tri = sb("tri", [P, P])
            ones = sb("ones", [P, P])
            slf = sb("slf", [P, 2, NT])
            slu = sb("slu", [P, 2, NT], U32)
            wsel = sb("wsel", [P, 2, NT])
            noop = sb("noop", [P, NT])

            def bc(v):
                return v.unsqueeze(2).to_broadcast(sh)

            with nc.Block() as block:
                @block.gpsimd
                def _(gp):
                    gp.memset(tri[:], 1.0).then_inc(sm["pchain"], 1)
                    gp.memset(ones[:], 1.0)
                    gp.wait_ge(sm["pchain"], 1)
                    gp.affine_select(out=tri[:], in_=tri[:], compare_op=ALU.is_ge, fill=0.0, base=0, pattern=[[1, P]], channel_multiplier=-1)
                    gp.iota(ebase[:], pattern=[[0, NT], [CAP, 8]], base=-1 - NE * CAP, channel_multiplier=0,
                            allow_small_or_imprecise_dtypes=True).then_inc(sm["setup"], 1)
                    gp.wait_ge(sm["route_i"], 1)
                    for t in range(NT):
                        for r in range(2):
                            gp.indirect_dma_start(moe_in, bass.IndirectOffsetOnAxis(ap=slu[:, r, t:t + 1], axis=0), xn[:, t, :], None,
                                                  bounds_check=NE * CAP - 1, oob_is_err=False).then_inc(sm["scat"], 16)
                    gp.wait_ge(sm["scat"], 16 * 2 * NT)

                @block.scalar
                def _(act):
                    act.wait_ge(sm["route_e"], 1)
                    act.activation(wts[:], tmp[:], ACT.Exp).then_inc(sm["sig_e"], 1)

                @block.tensor
                def _(pe):
                    pe.wait_ge(sm["route_m"], 1)
                    pe.wait_ge(sm["setup"], 1)
                    m2 = rmask[:].rearrange("p t e -> p (t e)")
                    pe.matmul(dn[0][:, 0:P], tri[:], m2, start=True, stop=True)
                    pe.matmul(dn[1][:, 0:P], ones[:], m2, start=True, stop=True).then_inc(sm["cum_ps"], 1)

                @block.vector
                def _(dve):
                    ch = Chain(dve, sm["chain"])
                    ch(dve.tensor_reduce(red[:], lg[:], AX.X, ALU.max))
                    dve.tensor_tensor(tmp[:], lg[:], bc(red[:]), ALU.subtract).then_inc(sm["route_e"], 1)
                    dve.wait_ge(sm["sig_e"], 1)
                    ch(dve.tensor_reduce(red[:], wts[:], AX.X, ALU.add))
                    ch(dve.reciprocal(red[:], red[:]))
                    ch(dve.tensor_tensor(wts[:], wts[:], bc(red[:]), ALU.mult))
                    ch(dve.memset(rank[:], 0.0))
                    for e in range(8):
                        ch(dve.tensor_tensor(tmp[:], bc(wts[:, :, e]), wts[:], ALU.is_gt))
                        ch(dve.tensor_tensor(rank[:], rank[:], tmp[:], ALU.add))
                        if e < 7:
                            tail = [P, NT, 7 - e]
                            ch(dve.tensor_tensor(tmp[:, :, e + 1:8], wts[:, :, e].unsqueeze(2).to_broadcast(tail), wts[:, :, e + 1:8], ALU.is_equal))
                            ch(dve.tensor_tensor(rank[:, :, e + 1:8], rank[:, :, e + 1:8], tmp[:, :, e + 1:8], ALU.add))
                    ch(dve.tensor_scalar(tmp[:], rank[:], 2.0, None, ALU.is_lt))
                    dve.scalar_tensor_tensor(rmask[:], wts[:], 0.0, tmp[:], ALU.is_gt, ALU.mult).then_inc(sm["route_m"], 1)
                    dve.wait_ge(sm["cum_ps"], 1)
                    ch(dve.memset(off[:, 0, :], 0.0))
                    for t in range(1, NT):
                        ch(dve.tensor_tensor(off[:, t, :], off[:, t - 1, :], dn[1][:, 8 * (t - 1):8 * t], ALU.add))
                    ch(dve.tensor_tensor(slot[:], off[:], dn[0][:, 0:P].rearrange("p (t e) -> p t e", e=8), ALU.add))
                    ch(dve.scalar_tensor_tensor(valid[:], slot[:], float(CAP), rmask[:], ALU.is_le, ALU.mult))
                    ch(dve.memset(valid[:, :, 7], 0.0))
                    ch(dve.tensor_tensor(noop[:], wts[:, :, 7], rmask[:, :, 7], ALU.mult))
                    dve.wait_ge(sm["setup"], 1)
                    ch(dve.tensor_tensor(slot[:], slot[:], ebase[:], ALU.add))
                    for r in range(2):
                        ch(dve.scalar_tensor_tensor(tmp[:], rank[:], float(r), valid[:], ALU.is_equal, ALU.mult))
                        ch(dve.tensor_tensor(off[:], tmp[:], wts[:], ALU.mult))
                        ch(dve.tensor_reduce(wsel[:, r, :], off[:], AX.X, ALU.add))
                        ch(dve.tensor_tensor(off[:], tmp[:], slot[:], ALU.mult))
                        ch(dve.tensor_reduce(slf[:, r, :], off[:], AX.X, ALU.add))
                    ch(dve.tensor_scalar(slf[:], slf[:], float(NE * CAP), None, ALU.add))
                    dve.tensor_copy(slu[:], slf[:]).then_inc(sm["route_i"], 1)
            clear()

            with ExitStack() as stE:
                scope.append(stE)
                raw_in = sb("raw_in", [P, KD, F])
                raw_out = sb("raw_out", [P, KF, D])
                ei = (sb("ei_hi", [P, KD, F], F32R), sb("ei_lo", [P, KD, F], F32R))
                eo = (sb("eo_hi", [P, KF, D], F32R), sb("eo_lo", [P, KF, D], F32R))
                xe = sb("xe", [P, TB, D])
                e_hi = sb("e_hi", [P, KF, S], F32R)
                e_lo = sb("e_lo", [P, KF, S], F32R)
                ye = sb("ye", [P, TB, D])
                with nc.Fori(0, NE) as e:
                    with nc.Block() as block:
                        @block.sync
                        def _(sp):
                            sp.dma_start(xe[:], moe_in[bass.ts(e, CAP), :].rearrange("(t p) d -> p t d", p=P)).then_inc(sm["x_ld"], 16)
                            for k in range(KD):
                                sp.dma_start(raw_in[:, k, :], ein[bass.ds(e * D + k * P, P), :]).then_inc(sm["ld"], 16)
                            for k in range(2):
                                sp.dma_start(raw_out[:, 4 * k:4 * k + 4, :], eout[bass.ds(e * F + k * 4 * P, 4 * P), :].rearrange("(k p) n -> p k n", p=P)).then_inc(sm["wsplit"], 16)
                            sp.wait_ge(sm["y_ready"], 1)
                            sp.dma_start(moe_out[bass.ts(e, CAP), :].rearrange("(t p) d -> p t d", p=P), ye[:]).then_inc(sm["st_x"], 16)
                            sp.wait_ge(sm["st_x"], 16)

                        @block.gpsimd
                        def _(gp):
                            gp.wait_ge(sm["w_free"], 1)
                            gp.wait_ge(sm["ld"], 32)
                            gp.tensor_tensor(ei[1][:, 0, :], raw_in[:, 0, :], ei[0][:, 0, :].bitcast(F32), ALU.subtract).then_inc(sm["raw_free"], 1)

                        @block.tensor
                        def _(pe):
                            pe.wait_ge(sm["x_ld"], 16)
                            pe_transpose(pe, dn[0], xe).then_inc(sm["hT_ps"], 1)
                            pe.wait_ge(sm["hT_ready"], 1)
                            pe.wait_ge(sm["raw_free"], 2)
                            for j, bank in enumerate((dn[1], dn[2], po, sc[0])):
                                for m in (2 * j, 2 * j + 1):
                                    for k in range(KD):
                                        last = mm3(pe, bank[:, (m % 2) * S:(m % 2 + 1) * S], [v[:, k, m * P:(m + 1) * P] for v in ei],
                                                   [hT_hi[:, k, :], hT_lo[:, k, :]], k == 0, k == KD - 1)
                                last.then_inc(sm["fc1_ps"], 1)
                            for t in range(TB):
                                for k in range(KF):
                                    if t == 0:
                                        pe.wait_ge(sm["hid_ready"], k // 2 + 1)
                                        if k % 4 == 0:
                                            pe.wait_ge(sm["setup"], k // 4 + 1)
                                    last = mm3(pe, sc[1][:, t * D:(t + 1) * D], [e_hi[:, k, t * P:(t + 1) * P], e_lo[:, k, t * P:(t + 1) * P]],
                                               [eo[0][:, k, :], eo[1][:, k, :]], k == 0, k == KF - 1)
                            last.then_inc(sm["fc2_ps"], 1)

                        @block.scalar
                        def _(act):
                            act.wait_ge(sm["ld"], 32)
                            act.activation(ei[0][:], raw_in[:], ACT.Copy).then_inc(sm["w_free"], 1)
                            act_h_T(act, 0)
                            for k in range(2):
                                act.wait_ge(sm["wsplit"], 32)
                                act.activation(eo[0][:, 4 * k:4 * k + 4, :], raw_out[:, 4 * k:4 * k + 4, :], ACT.Copy).then_inc(sm["w_free"], 1)
                            for j, bank in enumerate((dn[1], dn[2], po, sc[0])):
                                act.wait_ge(sm["fc1_ps"], j + 1)
                                act.activation(e_hi[:, 2 * j:2 * j + 2, :].rearrange("p k s -> p (k s)"), bank[:, :], ACT.Relu).then_inc(sm["hid_hi"], 1)

                        @block.vector
                        def _(dve):
                            dve.wait_ge(sm["w_free"], 1)
                            dve.wait_ge(sm["ld"], 32)
                            dve.tensor_tensor(ei[1][:, 1, :], raw_in[:, 1, :], ei[0][:, 1, :].bitcast(F32), ALU.subtract).then_inc(sm["raw_free"], 1)
                            dve_h_T(dve, 0)
                            for k in range(2):
                                dve.wait_ge(sm["w_free"], k + 2)
                                dve.wait_ge(sm["wsplit"], 32)
                                dve.tensor_tensor(eo[1][:, 4 * k:4 * k + 4, :], raw_out[:, 4 * k:4 * k + 4, :], eo[0][:, 4 * k:4 * k + 4, :].bitcast(F32),
                                                  ALU.subtract).then_inc(sm["setup"], 1)
                            for j, bank in enumerate((dn[1], dn[2], po, sc[0])):
                                dve.wait_ge(sm["hid_hi"], j + 1)
                                dve.scalar_tensor_tensor(e_lo[:, 2 * j:2 * j + 2, :].rearrange("p k s -> p (k s)"), bank[:, :], 0.0,
                                                         e_hi[:, 2 * j:2 * j + 2, :].rearrange("p k s -> p (k s)").bitcast(F32), ALU.max, ALU.subtract).then_inc(sm["hid_ready"], 1)
                            dve.wait_ge(sm["fc2_ps"], 1)
                            dve.tensor_copy(ye[:].rearrange("p t d -> p (t d)"), sc[1][:, :]).then_inc(sm["y_ready"], 1)
                    clear()
                scope.pop()

            with ExitStack() as stG:
                scope.append(stG)
                gat = sb("gat", [P, NT, 2, D])
                with nc.Block() as block:
                    @block.gpsimd
                    def _(gp):
                        for t in range(NT):
                            for r in range(2):
                                gp.indirect_dma_start(gat[:, t, r, :], None, moe_out, bass.IndirectOffsetOnAxis(ap=slu[:, r, t:t + 1], axis=0),
                                                      bounds_check=NE * CAP, oob_is_err=False).then_inc(sm[f"gath{t}"], 16)

                    @block.vector
                    def _(dve):
                        for t in range(NT):
                            dve.scalar_tensor_tensor(xres[:, t, :], xn[:, t, :], noop[:, t:t + 1], xres[:, t, :], ALU.mult, ALU.add).then_inc(sm["chain"], 1)
                        for r in range(2):
                            for t in range(NT):
                                dve.wait_ge(sm["chain"], NT * r + t + 1)
                                if r == 0:
                                    dve.wait_ge(sm[f"gath{t}"], 32)
                                dve.scalar_tensor_tensor(xres[:, t, :], gat[:, t, r, :], wsel[:, r, t:t + 1], xres[:, t, :], ALU.mult, ALU.add).then_inc(sm["chain"], 1)
                        dve.wait_ge(sm["chain"], 3 * NT)
                clear()
                scope.pop()
            scope.pop()

        with ExitStack() as stC:
            scope.append(stC)
            wq = [(sb(f"wC_hi{i}", [P, KD, D], F32R), sb(f"wC_lo{i}", [P, KD, D], F32R)) for i in range(4)]
            w1w = (sb("w1_hi", [P, KD, F], F32R), sb("w1_lo", [P, KD, F], F32R))
            w2w = (sb("w2_hi", [P, KF, D], F32R), sb("w2_lo", [P, KF, D], F32R))
            load_split([(wC[i].rearrange("(k p) n -> p k n", p=P), wq[i][0][:], wq[i][1][:]) for i in range(4)]
                       + [(w1.rearrange("(k p) n -> p k n", p=P), w1w[0][:], w1w[1][:]),
                          (w2.rearrange("(k p) n -> p k n", p=P), w2w[0][:], w2w[1][:])])
            LQ, LK, LV, LO = wq
            rows = sb("rowsC", [P, 4, D])
            cols = sb("colsC", [P, 2, KD])
            b1c = sb("b1c", [P, KF])
            g32 = sb("u32", [P, KF, K_SELECT])
            g_hi = sb("u_hi", [P, KF, K_SELECT], F32R)
            g_lo = sb("u_lo", [P, KF, K_SELECT], F32R)
            hn = sb("hn", [P, TB, D])
            score = sb("score", [P, TB])
            sig = sb("sig", [P, TB])
            spread = sb("spread", [P, TB, P])
            srow = sb("srow", [P, S])
            cmp = sb("cmp", [P, S])
            above = sb("above", [P, TB, 2])
            trank = sb("trank", [P, TB])
            infront = sb("infront", [P, TB, S])
            slot_no = sb("slot_no", [P, P])
            oh = sb("oh", [P, TB, P])
            ohT = sb("ohT", [P, TB, P])
            proc = sb("proc", [P, D])

            with nc.Block() as block:
                @block.sync
                def _(sp):
                    sp.dma_start(rows[:], rowC.unsqueeze(0).to_broadcast([P, 4, D])).then_inc(sm["ld"], 16)
                    sp.dma_start(cols[:], colC).then_inc(sm["ld"], 16)
                    sp.dma_start(b1c[:], b1).then_inc(sm["ld"], 16)

                @block.gpsimd
                def _(gp):
                    gp.memset(infront[:], 1.0).then_inc(sm["pchain"], 1)
                    gp.wait_ge(sm["pchain"], 1)
                    gp.affine_select(out=infront[:], in_=infront[:], compare_op=ALU.is_gt, fill=0.0, base=0, pattern=[[P, TB], [-1, S]], channel_multiplier=1)
                    gp.iota(slot_no[:], pattern=[[1, P]], base=0, channel_multiplier=0, allow_small_or_imprecise_dtypes=True)

                @block.vector
                def _(dve):
                    dve.wait_ge(sm["ld"], 48)
                    dve.tensor_scalar(cols[:, 0, :], cols[:, 0, :], float(1.0 / np.sqrt(DH)), None, ALU.mult).then_inc(sm["setup"], 1)
                    dve.wait_ge(sm["setup"], 1)
            clear()

            with nc.Fori(0, B) as b:
                with nc.Block() as block:
                    xb = xres[:, bass.ts(b, TB), :]

                    @block.sync
                    def _(sp):
                        sp.dma_start(ctx_raw[:], ctxT[bass.ts(b, 1), :, :].rearrange("o (k p) s -> p (o k) s", p=P)).then_inc(sm["ctx_ld"], 16)
                        sp_stack_all(sp, 0, "k", kstack[1])
                        sp_stack_all(sp, 0, "q", qstack)
                        sp_stack_max(sp, 0)
                        sp.wait_ge(sm["x_out"], 2)
                        sp.dma_start(out_t[:, bass.ts(b, TB), :], res[:]).then_inc(sm["st_out"], 16)
                        sp.wait_ge(sm["st_out"], 16)

                    @block.tensor
                    def _(pe):
                        pe.wait_ge(sm["ctx_split"], 1)
                        pe_project_T(pe, dn[1], LK, (c_hi, c_lo)).then_inc(sm["k_ps"], 1)
                        pe_project(pe, dn[2], LV, (c_hi, c_lo)).then_inc(sm["v_ps"], 1)
                        pe_h_T(pe, 0)
                        pe.wait_ge(sm["hT_ready"], 1)
                        pe_project_T(pe, dn[0], LQ, (hT_hi, hT_lo)).then_inc(sm["q_ps"], 1)
                        pe_attention(pe, 0, 0, kstack[1], LO)
                        pe.wait_ge(sm["route_e"], 1)
                        for t in range(TB):
                            last = pe.transpose(dn[1][:, t * P:(t + 1) * P], spread[:, t, :], ident[:])
                        last.then_inc(sm["srow_ps"], 1)
                        pe.wait_ge(sm["onehot"], 1)
                        for k in range(KD):
                            for t in range(TB):
                                last = pe.matmul(dn[0][:, k * P:(k + 1) * P], hn[:, t, k * P:(k + 1) * P], oh[:, t, :], start=(t == 0), stop=(t == TB - 1))
                        last.then_inc(sm["sel_ps"], 1)
                        for t in range(TB):
                            last = pe.transpose(dn[2][:, t * P:(t + 1) * P], oh[:, t, :], ident[:])
                        last.then_inc(sm["ohT_ps"], 1)
                        pe.wait_ge(sm["selT_ready"], 1)
                        for j in range(2):
                            for m in range(4 * j, 4 * j + 4):
                                for k in range(KD):
                                    last = mm3(pe, sc[j][:, (m % 4) * P:(m % 4 + 1) * P], [v[:, k, m * P:(m + 1) * P] for v in w1w],
                                               [hT_hi[:, k, 0:K_SELECT], hT_lo[:, k, 0:K_SELECT]], k == 0, k == KD - 1)
                            last.then_inc(sm["fc1_ps"], 1)
                        for k in range(KF):
                            pe.wait_ge(sm["hid_ready"], k + 1)
                            last = mm3(pe, sc[2][:, 0:D], [g_hi[:, k, :], g_lo[:, k, :]], [w2w[0][:, k, :], w2w[1][:, k, :]], k == 0, k == KF - 1)
                        last.then_inc(sm["fc2_ps"], 1)
                        pe.wait_ge(sm["proc_ready"], 1)
                        pe.wait_ge(sm["ohT_ready"], 1)
                        for t in range(TB):
                            last = pe.matmul(sc[3][:, t * D:(t + 1) * D], ohT[:, t, :], proc[:], start=True, stop=True)
                        last.then_inc(sm["upd_ps"], 1)

                    @block.scalar
                    def _(act):
                        act.wait_ge(sm["ctx_ld"], 16)
                        act.activation(c_hi[:], ctx_raw[:], ACT.Copy).then_inc(sm["ctx_hi"], 1)
                        act_qk(act, 0, "k", dn[1], cols[:, 1, :])
                        act_h_T(act, 0)
                        act_qk(act, 0, "q", dn[0], cols[:, 0, :])
                        act_attention(act, 0)
                        act.wait_ge(sm["route_e"], 1)
                        act.activation(sig[:], score[:], ACT.Exp, scale=-1.0).then_inc(sm["sig_e"], 1)
                        act.wait_ge(sm["ohT_ps"], 1)
                        act.activation(ohT[:].rearrange("p t s -> p (t s)"), dn[2][:, 0:TB * P], ACT.Copy).then_inc(sm["ohT_ready"], 1)
                        for m in range(KF):
                            act.wait_ge(sm["fc1_ps"], m // 4 + 1)
                            act.activation(g32[:, m, :], sc[m // 4][:, (m % 4) * P:(m % 4 + 1) * P], ACT.Gelu_apprx_tanh, bias=b1c[:, m:m + 1]).then_inc(sm["gelu"], 1)

                    @block.gpsimd
                    def _(gp):
                        pool_rstd(gp, 0)
                        gp.tensor_tensor(resb[:], xb, rows[:, R_LO, :].unsqueeze(1).to_broadcast([P, TB, D]), ALU.add).then_inc(sm["resb_ready"], 1)
                        pool_rstd(gp, 1)
                        for m in range(KF):
                            gp.wait_ge(sm["gelu"], m + 1)
                            gp.tensor_copy(g_hi[:, m, :], g32[:, m, :]).then_inc(sm["hid_hi"], 1)

                    @block.vector
                    def _(dve):
                        ch = Chain(dve, sm["chain"])
                        dve_norm(dve, ch, 0, xb)
                        dve_norm_apply(dve, xb, h).then_inc(sm["h_ready"], 1)
                        dve.wait_ge(sm["ctx_hi"], 1)
                        dve.tensor_tensor(c_lo[:], ctx_raw[:], c_hi[:].bitcast(F32), ALU.subtract).then_inc(sm["ctx_split"], 1)
                        dve_h_T(dve, 0)
                        dve_qkv(dve, ch, 0, rows[:, R_LV, :])
                        dve_attention(dve, ch, 0)
                        dve.wait_ge(sm["op_ps"], 1)
                        dve.wait_ge(sm["resb_ready"], 1)
                        ch(dve.tensor_tensor(res[:].rearrange("p t d -> p (t d)"), dn[0][:, :], resb[:].rearrange("p t d -> p (t d)"), ALU.add))
                        dve_norm(dve, ch, 1, res)
                        ch(dve_norm_apply(dve, res, hn))
                        for t in range(TB):
                            ch(dve.tensor_tensor_reduce(norm[:, t, :], hn[:, t, :], rows[:, R_RT, :], 1.0, 0.0, ALU.mult, ALU.add, score[:, t:t + 1]))
                        dve.tensor_copy(spread[:], score[:].unsqueeze(2).to_broadcast([P, TB, P])).then_inc(sm["route_e"], 1)
                        ch(dve.tensor_tensor(res[:], res[:], hn[:], ALU.add))
                        dve.wait_ge(sm["srow_ps"], 1)
                        ch(dve.tensor_copy(srow[:], dn[1][:, 0:S]))
                        for t in range(TB):
                            ch(dve.tensor_scalar(cmp[:], srow[:], score[:, t:t + 1], None, ALU.is_gt, ALU.add, accum_out=above[:, t, 0:1]))
                            ch(dve.scalar_tensor_tensor(cmp[:], srow[:], score[:, t:t + 1], infront[:, t, :], ALU.is_equal, ALU.mult, accum_out=above[:, t, 1:2]))
                        ch(dve.tensor_tensor(trank[:], above[:, :, 0], above[:, :, 1], ALU.add))
                        for t in range(TB):
                            last = dve.tensor_scalar(oh[:, t, :], slot_no[:], trank[:, t:t + 1], None, ALU.is_equal)
                        last.then_inc(sm["onehot"], 1)
                        dve.wait_ge(sm["sig_e"], 1)
                        ch(dve.tensor_scalar(sig[:], sig[:], 1.0, None, ALU.add))
                        ch(dve.reciprocal(sig[:], sig[:]))
                        dve.wait_ge(sm["sel_ps"], 1)
                        sel = dn[0][:, 0:KD * P].rearrange("p (k s) -> p k s", k=KD)
                        ch(dve.tensor_copy(hT_hi[:, :, 0:K_SELECT], sel))
                        dve.tensor_tensor(hT_lo[:, :, 0:K_SELECT], sel, hT_hi[:, :, 0:K_SELECT].bitcast(F32), ALU.subtract).then_inc(sm["selT_ready"], 1)
                        for m in range(KF):
                            dve.wait_ge(sm["hid_hi"], m + 1)
                            dve.tensor_tensor(g_lo[:, m, :], g32[:, m, :], g_hi[:, m, :].bitcast(F32), ALU.subtract).then_inc(sm["hid_ready"], 1)
                        dve.wait_ge(sm["fc2_ps"], 1)
                        dve.tensor_tensor(proc[:], sc[2][:, 0:D], rows[:, R_B2, :], ALU.add).then_inc(sm["proc_ready"], 1)
                        dve.wait_ge(sm["upd_ps"], 1)
                        for t in range(TB):
                            last = dve.scalar_tensor_tensor(res[:, t, :], sc[3][:, t * D:(t + 1) * D], sig[:, t:t + 1], res[:, t, :], ALU.mult, ALU.add)
                            last.then_inc(sm["x_out"], 1)
                        dve.wait_ge(sm["x_out"], 2)
                clear()
            scope.pop()


def kernel(**inputs):
    import numpy as _np
    import concourse.bacc as _bacc
    from concourse import mybir as _mybir
    from concourse.bass_utils import run_bass_kernel_spmd as _run

    g = {k: _np.asarray(v) for k, v in inputs.items()}

    def head_cols(w):
        return w.reshape(-1, 2, HG, DH).transpose(0, 1, 3, 2).reshape(w.shape)

    def head_col_bias(v):
        return v.reshape(2, HG, DH).transpose(2, 1, 0).reshape(P, 2)

    def col(v):
        return v.reshape(-1, P).T

    a, c = "L0_xattn_", "L1_xattn_"
    data = {
        "x": g["x"].reshape(B * S, D),
        "ctxT": g["ctx_1024"].transpose(0, 2, 1),
        "mask": g["mask_Bx1x1xS2_ff0"].reshape(B, S),
        "wA": _np.stack([head_cols(g[a + "cq_w"]), head_cols(g[a + "ck_w"]), g[a + "cv_w"], g[a + "co_w"],
                         head_cols(g[a + "sq_w"]), head_cols(g[a + "sk_w"]), g[a + "sv_w"], g[a + "so_w"]]),
        "colA": _np.stack([head_col_bias(g[a + n]) for n in ("cq_b", "ck_b", "sq_b", "sk_b")], axis=1),
        "rowA": _np.stack([g[a + n] for n in ("cv_b", "co_b", "co_g", "co_be", "sv_b", "so_b", "so_g", "so_be", "fo_b", "fo_g", "fo_be")]),
        "fi": g[a + "fi_w"], "fo": g[a + "fo_w"], "fib": col(g[a + "fi_b"]),
        "rw": g["L0_ffn_router_w"].T, "rb": g["L0_ffn_router_b"].reshape(1, 8),
        "ein": g["L0_ffn_experts_inter"].reshape(NE * D, F), "eout": g["L0_ffn_experts_out"].reshape(NE * F, D),
        "wC": _np.stack([head_cols(g[c + "W_q"].T), head_cols(g[c + "W_k"].T), g[c + "W_v"].T, g[c + "W_o"].T]),
        "colC": _np.stack([head_col_bias(g[c + n]) for n in ("b_q", "b_k")], axis=1),
        "rowC": _np.stack([g[c + "b_v"], g[c + "b_o"], g["L1_ffn_b2"], g["L1_ffn_w_router"]]),
        "w1": g["L1_ffn_W1"], "w2": g["L1_ffn_W2"], "b1": col(g["L1_ffn_b1"]),
    }
    nc = _bacc.Bacc("TRN2", target_bir_lowering=False, num_devices=1)
    arrays, args = {}, []
    for name, v in data.items():
        v = _np.ascontiguousarray(v)
        arrays[f"in_{name}"] = v
        args.append(nc.dram_tensor(f"in_{name}", v.shape, _mybir.dt.from_np(v.dtype), kind="ExternalInput").ap())
    args.append(nc.dram_tensor("out_0", (B * S, D), F32, kind="ExternalOutput").ap())
    build(nc, *args)
    r = _run(nc, [arrays], core_ids=[0])
    return r.results[0]["out_0"].reshape(B, S, D)
```

```python
from contextlib import ExitStack

import concourse.bass as bass
import numpy as np
from concourse import mybir

F32 = mybir.dt.float32
F32R = mybir.dt.float32r
U32 = mybir.dt.uint32
ACT = mybir.ActivationFunctionType
ALU = mybir.AluOpType
AX = mybir.AxisListType

P = 128
B, S, D, H = 8, 256, 256, 16
DH = D // H
NT = B * S // P
TB = S // P
KD = D // P
HG = H // 2
F = 1024
KF = F // P
NE = 7
CAP = B * S // 8
K_SELECT = S // 2
EPS = 1e-5
MASK_ROW = 3 * DH
MAX_ROW = MASK_ROW + 2
SROWS = MASK_ROW + 2
STROWS = MAX_ROW + 1
NBANK = 2
NPT = 8
NS = 2
LAG = 20

(R_CV, R_CO, R_CG, R_CBE, R_SV, R_SO, R_SG, R_SBE, R_FO, R_FG, R_FBE) = range(11)
(R_LV, R_LO, R_B2, R_RT) = range(4)


class Chain:

    def __init__(self, eng, sem):
        self.eng, self.sem, self.n = eng, sem, 0

    def __call__(self, ins):
        self.n += 1
        ins.then_inc(self.sem, 1)
        self.eng.wait_ge(self.sem, self.n)


def side_by_side(*programs):
    waiting = [(next(p), n, p) for n, p in enumerate(programs)]
    while waiting:
        step, n, p = min(waiting, key=lambda w: w[:2])
        waiting.remove((step, n, p))
        try:
            waiting.append((next(p), n, p))
        except StopIteration:
            pass


def build(nc, x, ctxT, mask, wA, colA, rowA, fi, fo, fib, rw, rb, ein, eout, wC, colC, rowC, w1, w2, b1, out):
    moe_in = nc.dram_tensor("moe_in", [NE * CAP, D], F32, kind="Internal").ap()
    moe_out = nc.dram_tensor("moe_out", [NE * CAP + 1, D], F32, kind="Internal").ap()
    xn_dram = nc.dram_tensor("xn_dram", [B * S, D], F32, kind="Internal").ap()
    mask_dram = nc.dram_tensor("mask_dram", [B + 1, 2, HG, S], F32, kind="Internal").ap()
    xn_t = xn_dram.rearrange("(t p) d -> p t d", p=P)
    x_t = x.rearrange("(t p) d -> p t d", p=P)
    out_t = out.rearrange("(t p) d -> p t d", p=P)

    root = ExitStack()
    scope = [root]

    def sb(name, shape, dt=F32):
        return scope[-1].enter_context(nc.sbuf_tensor(name, shape, dt))

    def sem(name):
        return scope[-1].enter_context(nc.semaphore(name))

    with root:
        banks = [root.enter_context(nc.psum_tensor(f"bank{i}", [P, 512], F32)) for i in range(8)]

        xres = sb("xres", [P, NT, D])
        ident = sb("ident", [P, P])
        half = sb("half", [P, 2])

        class Slot:

            def __init__(self, n):
                def b(name, shape, dt=F32):
                    return sb(f"{name}_{n}", shape, dt)

                self.n = n
                self.t0 = n * LAG
                self.sc = banks[4 * n:4 * n + 2]
                self.dn = banks[4 * n + 2:4 * n + 4]
                self.qstack = b("qstack", [P, HG, S], F32R)
                self.kstack = b("kstack", [P, HG, S], F32R)
                self.vext = b("vext", [P, TB, H, 2 * DH])
                self.ctx_raw = b("ctx_raw", [P, KD, S])
                self.hT_hi = b("hT_hi", [P, KD, S], F32R)
                self.hT_lo = b("hT_lo", [P, KD, S], F32R)
                self.q_parts = b("q_parts", [P, 2, 2, S], F32R)
                self.q_hi, self.q_lo = self.q_parts[:, 0], self.q_parts[:, 1]
                self.c_hi, self.c_lo = self.hT_hi[:], self.hT_lo[:]
                self.k_parts = b("k_parts", [P, 2, 2, S], F32R)
                self.k_hi, self.k_lo = self.k_parts[:, 0], self.k_parts[:, 1]
                self.nmax = b("nmax", [P, 2, TB, HG])
                self.m_hi = b("m_hi", [HG, 2, S], F32R)
                self.probs = b("probs", [P, NPT - 2, TB, S])
                q_heads = self.q_parts[:].bitcast(F32)
                self.head_probs = [*(self.probs[:, i] for i in range(NPT - 2)), q_heads[:, 0], q_heads[:, 1]]
                self.oext = self.k_parts[:].rearrange("p a m s -> p (a m) s").bitcast(F32)
                self.rsum = b("rsum", [P, TB, H])
                self.h = b("h", [P, TB, D])
                self.res = b("res", [P, TB, D])
                self.resb = b("resb", [P, TB, D])
                self.norm = b("norm", [P, TB, D])
                self.attn = self.norm
                self.bn = b("bn", [P, TB, 6])
                self.mv = b("mv", [P, TB, 2])
                self.var = b("var", [P, TB])
                self.rstd = b("rstd", [P, TB])
                self.sm = {k: sem(f"{k}_{n}") for k in SLOT_SEMS}

        SLOT_SEMS = """ones_s stk_mask ctx_ld ctx_hi ctx_split h_ready hT_ps hT_hi_s hT_ready
            k_ps q_ps v_ps k_hi_s q_hi_s k_split q_split v_ready stk_k stk_q s_ps s_max mT_ps m_row stk_m0 stk_m1
            st_ps exp_done pv_ps o_ev oT_ps o_norm o2_ps o2_hi o2_ready op_ps resb_ready ln_var ln_rstd
            chain fc1_ps gelu hid_hi hid_ready fc2_ps log_ps st_x""".split()
        LATE_SEMS = """route_e srow_ps onehot sel_ps selT_ready ohT_ps ohT_ready proc_ready upd_ps x_out st_out sig_e""".split()
        names = """ld wsplit setup hT_ps hT_hi_s hT_ready chain pchain fc1_ps hid_hi hid_ready fc2_ps st_x raw_free route_e route_m
            cum_ps route_i wload0 wload1 scat w_free y_ready x_ld sig_e""".split()
        sm = {n: sem(n) for n in names}
        slots = [Slot(n) for n in range(NS)]
        sc, dn, po = banks[0:2], banks[2:5], banks[5]
        hT_hi, hT_lo = slots[0].hT_hi, slots[0].hT_lo
        probs2 = [s.probs[:, 0:4].rearrange("p a t s -> p (a t s)") for s in slots]

        def clear():
            nums = sorted(v.num for v in [*sm.values(), *(v for s in slots for v in s.sm.values())])
            first = nums[0]
            for n, after in zip(nums, [*nums[1:], None]):
                if after != n + 1:
                    nc.gpsimd.sem_clear(range(first, n + 1))
                    first = after
            nc.all_engine_barrier()

        def mm3(pe, dst, lhs, rhs, first, last):
            pe.matmul(dst, lhs[0], rhs[0], start=first, stop=False)
            pe.matmul(dst, lhs[1], rhs[0], start=False, stop=False)
            return pe.matmul(dst, lhs[0], rhs[1], start=False, stop=last)

        def pe_project_T(pe, dst, w, src):
            for m in range(KD):
                for k in range(KD):
                    last = mm3(pe, dst[:, m * S:(m + 1) * S],
                               [v[:, k, m * P:(m + 1) * P] for v in w], [v[:, k, :] for v in src], k == 0, k == KD - 1)
            return last

        def pe_project(pe, dst, w, src):
            for t in range(TB):
                for k in range(KD):
                    last = mm3(pe, dst[:, t * D:(t + 1) * D],
                               [v[:, k, t * P:(t + 1) * P] for v in src], [v[:, k, :] for v in w], k == 0, k == KD - 1)
            return last

        def pe_transpose(pe, dst, src):
            for k in range(KD):
                for t in range(TB):
                    last = pe.transpose(dst[:, k * S + t * P:k * S + (t + 1) * P], src[:, t, k * P:(k + 1) * P], ident[:])
            return last

        def pe_h_T(pe, sl, n, t):
            yield t
            pe.wait_ge(sl.sm["h_ready"], n + 1)
            pe_transpose(pe, sl.dn[0], sl.h).then_inc(sl.sm["hT_ps"], 1)

        def act_h_T(act, sl, n, t):
            yield t + 0.7
            act.wait_ge(sl.sm["hT_ps"], n + 1)
            act.activation(sl.hT_hi[:].rearrange("p k s -> p (k s)"), sl.dn[0][:, :], ACT.Copy).then_inc(sl.sm["hT_hi_s"], 1)

        def dve_h_T(dve, sl, n, t):
            yield t + 1.3
            dve.wait_ge(sl.sm["hT_hi_s"], n + 1)
            dve.tensor_tensor(sl.hT_lo[:].rearrange("p k s -> p (k s)"), sl.dn[0][:, :],
                              sl.hT_hi[:].rearrange("p k s -> p (k s)").bitcast(F32), ALU.subtract).then_inc(sl.sm["hT_ready"], 1)

        T_FIRST, T_SECOND, T_OUT, T_END = 0, 14, 27, 36
        HEAD = 0.6

        def pe_attention(pe, sl, a, t0, nxt):
            sm, sc, dn, qst, kst = sl.sm, sl.sc, sl.dn, sl.qstack, sl.kstack
            yield t0
            pe.wait_ge(sm["stk_k"], 96 * (a + 1))
            pe.wait_ge(sm["stk_q"], 96 * (a + 1))
            pe.wait_ge(sm["stk_mask"], 32 * (a + 1))

            def max_T(j):
                yield t0 + T_FIRST + HEAD * (HG * (j + 1) + 1.6)
                pe.wait_ge(sm["s_max"], H * a + HG * (j + 1))
                if j == 0:
                    pe.wait_ge(sm["k_split"], a + 1)
                else:
                    pe.wait_ge(sm["v_ready"], a + 1)
                for t in range(TB):
                    last = pe.transpose(dn[j][0:HG, t * P:(t + 1) * P], sl.nmax[:, j, t, :], ident[:])
                last.then_inc(sm["mT_ps"], 1)

            def pv(u):
                yield t0 + T_SECOND + HEAD * (4 * u + 5.6)
                pe.wait_ge(sm["exp_done"], H * a + 4 * u + 4)
                if u >= 2:
                    pe.wait_ge(sm["o_ev"], 4 * a + u - 1)
                for t in range(TB):
                    for j in range(4):
                        i = 4 * u + j
                        head = (i % 2) * HG + i // 2
                        last = pe.matmul(dn[u % 2][32 * j:32 * j + 32, 0:S], sl.vext[:, t, head, :],
                                         sl.head_probs[i % NPT][:, t, :], start=(t == 0), stop=(t == TB - 1),
                                         tile_position=(0, 32 * j), skip_group_check=True)
                last.then_inc(sm["pv_ps"], 1)

            for i in range(H):
                yield t0 + T_FIRST + HEAD * i
                g, s = i // 2, i % 2
                if i >= NBANK:
                    pe.wait_ge(sm["s_max"], H * a + i - NBANK + 1)
                for t in range(TB):
                    last = pe.matmul(sc[i % NBANK][:, t * S:(t + 1) * S], qst[64 * s:64 * s + SROWS, g, t * P:(t + 1) * P],
                                     kst[64 * s:64 * s + SROWS, g, :], start=True, stop=True)
                last.then_inc(sm["s_ps"], 1)
                if i == HG + 1:
                    yield from max_T(0)
            yield from max_T(1)
            for i in range(H):
                yield t0 + T_SECOND + HEAD * i
                g, s = i // 2, i % 2
                if i < NBANK:
                    pe.wait_ge(sm["s_max"], H * a + H - NBANK + i + 1)
                else:
                    pe.wait_ge(sm["exp_done"], H * a + i - NBANK + 1)
                if i % HG == 0:
                    pe.wait_ge(sm[f"stk_m{i // HG}"], 32 * (a + 1))
                for t in range(TB):
                    last = pe.matmul(sc[i % NBANK][:, t * S:(t + 1) * S], kst[64 * s:64 * s + STROWS, g, t * P:(t + 1) * P],
                                     qst[64 * s:64 * s + STROWS, g, :], start=True, stop=True)
                last.then_inc(sm["st_ps"], 1)
                if i % 4 == 1 and i > 4:
                    yield from pv(i // 4 - 1)
            yield from pv(3)
            yield t0 + T_OUT
            pe.wait_ge(sm["o_ev"], 4 * a + 4)
            for t in range(TB):
                for u in range(4):
                    last = pe.transpose(dn[t][:, u * P:(u + 1) * P], sl.oext[:, u, t * P:(t + 1) * P], ident[:])
                last.then_inc(sm["oT_ps"], 1)
            yield t0 + T_OUT + 3
            pe.wait_ge(sm["o_norm"], a + 1)
            pe_transpose(pe, sc[0], sl.attn).then_inc(sm["o2_ps"], 1)
            yield t0 + T_OUT + 5.5
            pe.wait_ge(sm["o2_ready"], a + 1)
            pe_project(pe, dn[0], nxt, (sl.hT_hi, sl.hT_lo)).then_inc(sm["op_ps"], 1)

        def act_qk(act, sl, a, which, bank, col, t):
            yield t
            dst = sl.q_hi if which == "q" else sl.k_hi
            act.wait_ge(sl.sm[f"{which}_ps"], a + 1)
            for m in range(KD):
                last = act.activation(dst[:, m, :], bank[:, m * S:(m + 1) * S], ACT.Identity, bias=col[:, m:m + 1])
            last.then_inc(sl.sm[f"{which}_hi_s"], 1)

        def act_attention(act, sl, a, t0):
            for i in range(H):
                yield t0 + T_SECOND + HEAD * (i + 0.5)
                act.wait_ge(sl.sm["st_ps"], H * a + i + 1)
                if i >= NPT:
                    act.wait_ge(sl.sm["pv_ps"], 4 * a + (i - NPT) // 4 + 1)
                act.activation(sl.head_probs[i % NPT].rearrange("p t s -> p (t s)"), sl.sc[i % NBANK][:, :], ACT.Exp).then_inc(sl.sm["exp_done"], 1)
            yield t0 + T_OUT + 4
            act.wait_ge(sl.sm["o2_ps"], a + 1)
            act.activation(sl.hT_hi[:].rearrange("p k s -> p (k s)"), sl.sc[0][:, :], ACT.Copy).then_inc(sl.sm["o2_hi"], 1)

        def dve_qk(dve, sl, a, which, bank, col, t):
            yield t
            hi, lo = (sl.q_hi, sl.q_lo) if which == "q" else (sl.k_hi, sl.k_lo)
            dve.wait_ge(sl.sm[f"{which}_hi_s"], a + 1)
            for m in range(KD):
                last = dve.scalar_tensor_tensor(lo[:, m, :], bank[:, m * S:(m + 1) * S], col[:, m:m + 1], hi[:, m, :].bitcast(F32),
                                                ALU.add, ALU.subtract)
            last.then_inc(sl.sm[f"{which}_split"], 1)

        def dve_v(dve, sl, a, vrow, t0):
            yield t0
            dve.wait_ge(sl.sm["v_ps"], a + 1)
            for t in range(TB):
                last = dve.tensor_tensor(sl.vext[:, t, :, 0:DH], sl.dn[1][:, t * D:(t + 1) * D].rearrange("p (h d) -> p h d", d=DH),
                                         vrow.rearrange("p (h d) -> p h d", d=DH), ALU.add)
            last.then_inc(sl.sm["v_ready"], 1)

        def dve_attention(dve, ch, sl, a, t0):
            sm, sc, dn = sl.sm, sl.sc, sl.dn

            def max_row(j):
                yield t0 + T_FIRST + HEAD * (HG * (j + 1) + 2.2)
                dve.wait_ge(sm["mT_ps"], 2 * a + j + 1)
                dve.tensor_copy(sl.m_hi[:, j, :], dn[j][0:HG, 0:S]).then_inc(sm["m_row"], 1)

            for i in range(H):
                yield t0 + T_FIRST + HEAD * (i + 0.5)
                j, slot = i // HG, (i % 2) * (HG // 2) + (i % HG) // 2
                dve.wait_ge(sm["s_ps"], H * a + i + 1)
                dve.tensor_reduce(sl.nmax[:, j, :, slot], sc[i % NBANK][:, :].rearrange("p (t s) -> p t s", t=TB), AX.X, ALU.max,
                                  negate=True).then_inc(sm["s_max"], 1)
                if i == HG + 1:
                    yield from max_row(0)
            yield from max_row(1)
            for u in range(4):
                yield t0 + T_SECOND + HEAD * (4 * u + 7.2)
                dve.wait_ge(sm["pv_ps"], 4 * a + u + 1)
                dve.tensor_copy(sl.oext[:, u, :], dn[u % 2][:, 0:S]).then_inc(sm["o_ev"], 1)
            for t in range(TB):
                yield t0 + T_OUT + 1 + t
                dve.wait_ge(sm["oT_ps"], 2 * a + t + 1)
                grp = dn[t][:, :].rearrange("p (g s e) -> p g s e", s=2, e=2 * DH)
                ch(dve.reciprocal(sl.rsum[:, t, :].rearrange("p (g s) -> p g s", s=2), grp[:, :, :, DH]))
                last = dve.tensor_tensor(sl.attn[:, t, :].rearrange("p (s g d) -> p g s d", s=2, g=HG), grp[:, :, :, 0:DH],
                                         sl.rsum[:, t, :].rearrange("p (g s) -> p g s", s=2).unsqueeze(3).to_broadcast([P, HG, 2, DH]), ALU.mult)
            last.then_inc(sm["o_norm"], 1)
            yield t0 + T_OUT + 5
            dve.wait_ge(sm["o2_hi"], a + 1)
            dve.tensor_tensor(sl.hT_lo[:].rearrange("p k s -> p (k s)"), sc[0][:, :],
                              sl.hT_hi[:].rearrange("p k s -> p (k s)").bitcast(F32), ALU.subtract).then_inc(sm["o2_ready"], 1)

        def dve_norm(dve, ch, sl, n, src, t0):
            yield t0
            for t in range(TB):
                last = dve.bn_stats(sl.bn[:, t, :], src[:, t, :])
            ch(last)
            for t in range(TB):
                last = dve.bn_aggr(sl.mv[:, t, :], sl.bn[:, t, :])
            ch(last)
            dve.tensor_scalar(sl.var[:, :], sl.mv[:, :, 1], EPS, None, ALU.add).then_inc(sl.sm["ln_var"], 1)
            yield t0 + 1.8
            dve.wait_ge(sl.sm["ln_rstd"], n + 1)

        def dve_norm_apply(dve, sl, src, dst):
            for t in range(TB):
                last = dve.tensor_scalar(dst[:, t, :], src[:, t, :], sl.mv[:, t, 0:1], sl.rstd[:, t:t + 1], ALU.subtract, ALU.mult)
            return last

        def dve_affine(dve, ch, sl, g, be, dst):
            ch(dve.tensor_tensor(sl.norm[:], sl.norm[:], g.unsqueeze(1).to_broadcast([P, TB, D]), ALU.mult))
            return dve.tensor_tensor(dst, sl.norm[:], be, ALU.add)

        def pool_rstd(gp, sl, n, t0):
            yield t0 + 1
            gp.wait_ge(sl.sm["ln_var"], n + 1)
            gp.tensor_tensor(sl.rstd[:, :], sl.var[:, :], half[:, :], ALU.pow).then_inc(sl.sm["ln_rstd"], 1)

        def pool_ones(gp, sl, t0):
            yield t0
            for stack in (sl.kstack, sl.qstack):
                gp.memset(stack[:].bitcast(F32), 1.0).then_inc(sl.sm["ones_s"], 1)

        def sp_stack(sp, sl, a, which, t0):
            yield t0
            parts, dst = ((sl.q_hi, sl.q_hi, sl.q_lo), sl.qstack) if which == "q" else ((sl.k_hi, sl.k_lo, sl.k_hi), sl.kstack)
            sp.wait_ge(sl.sm[f"{which}_split"], a + 1)
            sp.wait_ge(sl.sm["ones_s"], 2)
            for s in range(2):
                for c in range(3):
                    sp.dma_start(dst[64 * s + DH * c:64 * s + DH * (c + 1), :, :].bitcast(F32), parts[c][:, s, :].bitcast(F32)).then_inc(sl.sm[f"stk_{which}"], 16)

        def sp_stack_max(sp, sl, a, t0):
            for j in range(2):
                yield t0 + T_FIRST + HEAD * (HG * (j + 1) + 3)
                sp.wait_ge(sl.sm["m_row"], 2 * a + j + 1)
                for s in range(2):
                    sp.dma_start(sl.qstack[64 * s + MAX_ROW:64 * s + MAX_ROW + 1, 4 * j:4 * j + 4, :].bitcast(F32),
                                 sl.m_hi[4 * s:4 * s + 4, j, :].bitcast(F32)).then_inc(sl.sm[f"stk_m{j}"], 16)

        def sp_mask(sp, sl, a, src, t0):
            yield t0
            sp.wait_ge(sl.sm["ones_s"], 2)
            if a:
                sp.wait_ge(sl.sm["op_ps"], a)
            for s in range(2):
                sp.dma_start(sl.kstack[64 * s + MASK_ROW:64 * s + MASK_ROW + 2, :, :].bitcast(F32), src).then_inc(sl.sm["stk_mask"], 16)

        def load_split(weights):
            stage = probs2
            if True:
                with nc.Block() as block:
                    @block.sync
                    def _(sp):
                        for i, (src, hi, lo, scale) in enumerate(weights):
                            if i >= 2:
                                sp.wait_ge(sm["raw_free"], i - 1)
                            n = src.shape[1] * src.shape[2]
                            sp.dma_start(stage[i % 2][:, 0:n].rearrange("p (a b) -> p a b", a=src.shape[1]), src).then_inc(sm[f"wload{i % 2}"], 16)

                    @block.vector
                    def _(dve):
                        for i, (src, hi, lo, scale) in enumerate(weights):
                            n = src.shape[1] * src.shape[2]
                            raw = stage[i % 2][:, 0:n].rearrange("p (a b) -> p a b", a=src.shape[1])
                            dve.wait_ge(sm[f"wload{i % 2}"], 16 * (i // 2 + 1))
                            dve.tensor_scalar(hi, raw, scale, None, ALU.mult).then_inc(sm["w_free"], 1)
                            dve.wait_ge(sm["w_free"], i + 1)
                            dve.scalar_tensor_tensor(lo, raw, scale, hi.bitcast(F32), ALU.mult, ALU.subtract).then_inc(sm["raw_free"], 1)
                clear()

        lg = sb("lg", [P, NT, 8])

        QSCALE = float(1.0 / np.sqrt(DH))
        with ExitStack() as st0:
            zeros = st0.enter_context(nc.sbuf_tensor("zeros", [P, NE * CAP // P, D], F32))
            mrow = st0.enter_context(nc.sbuf_tensor("mrow", [B, S], F32))
            mhl = st0.enter_context(nc.sbuf_tensor("mhl", [B, 2, S], F32R))
            with nc.Block() as block:
                @block.sync
                def _(sp):
                    sp.dma_start(mrow[:], mask).then_inc(sm["x_ld"], 16)
                    sp.dma_start(xres[:], x_t).then_inc(sm["ld"], 16)
                    sp.wait_ge(sm["setup"], 2)
                    sp.dma_start(moe_in.rearrange("(t p) d -> p t d", p=P), zeros[:]).then_inc(sm["ld"], 16)
                    sp.dma_start(moe_out[NE * CAP:NE * CAP + 1, :], zeros[0:1, 0, :]).then_inc(sm["ld"], 16)
                    sp.dma_start(mask_dram[B].rearrange("c g s -> c (g s)"), zeros[0:2, 0:8, :].rearrange("p a d -> p (a d)")).then_inc(sm["ld"], 16)
                    sp.wait_ge(sm["raw_free"], 1)
                    for g in range(HG):
                        sp.dma_start(mask_dram[0:B, :, g, :], mhl[:].bitcast(F32)).then_inc(sm["ld"], 16)
                    sp.wait_ge(sm["ld"], 16 * (4 + HG))

                @block.gpsimd
                def _(gp):
                    gp.memset(ident[:], 0.0).then_inc(sm["pchain"], 1)
                    gp.memset(half[:], -0.5)
                    gp.wait_ge(sm["pchain"], 1)
                    gp.affine_select(out=ident[:], in_=ident[:], compare_op=ALU.not_equal, fill=1.0, base=0,
                                     pattern=[[-1, P]], channel_multiplier=1)
                    for sl in slots:
                        gp.memset(sl.vext[:], 1.0)

                @block.vector
                def _(dve):
                    ch = Chain(dve, sm["chain"])
                    dve.memset(zeros[:, 0:7, :], 0.0).then_inc(sm["setup"], 1)
                    dve.memset(zeros[:, 7:14, :], 0.0).then_inc(sm["setup"], 1)
                    dve.wait_ge(sm["x_ld"], 16)
                    ch(dve.tensor_scalar(mrow[:], mrow[:], -3.0e38, None, ALU.max))
                    ch(dve.tensor_copy(mhl[:, 0, :], mrow[:]))
                    dve.tensor_tensor(mhl[:, 1, :], mrow[:], mhl[:, 0, :].bitcast(F32), ALU.subtract).then_inc(sm["raw_free"], 1)
            clear()

        with ExitStack() as stA:
            scope.append(stA)
            wq = [(sb(f"wA_hi{i}", [P, KD, D], F32R), sb(f"wA_lo{i}", [P, KD, D], F32R)) for i in range(8)]
            fiw = (sb("fi_hi", [P, KD, F], F32R), sb("fi_lo", [P, KD, F], F32R))
            fow = (sb("fo_hi", [P, KF, D], F32R), sb("fo_lo", [P, KF, D], F32R))
            rww = (sb("rw_hi", [P, KD, 8], F32R), sb("rw_lo", [P, KD, 8], F32R))
            load_split([(wA[i].rearrange("(k p) n -> p k n", p=P), wq[i][0][:], wq[i][1][:], QSCALE if i in (0, 4) else 1.0) for i in range(8)]
                       + [(fi.rearrange("(k p) n -> p k n", p=P), fiw[0][:], fiw[1][:], 1.0),
                          (fo.rearrange("(k p) n -> p k n", p=P), fow[0][:], fow[1][:], 1.0),
                          (rw.rearrange("(k p) n -> p k n", p=P), rww[0][:], rww[1][:], 1.0)])
            rows = sb("rowsA", [P, 11, D])
            cols = sb("colsA", [P, 4, KD])
            fibc = sb("fib", [P, KF])
            rbr = sb("rbr", [P, 8])
            CQ, CK, CV, CO, SQ, SK, SV, SO = wq

            with nc.Block() as block:
                @block.sync
                def _(sp):
                    sp.dma_start(rows[:], rowA.unsqueeze(0).to_broadcast([P, 11, D])).then_inc(sm["ld"], 16)
                    sp.dma_start(cols[:], colA).then_inc(sm["ld"], 16)
                    sp.dma_start(fibc[:], fib).then_inc(sm["ld"], 16)
                    sp.dma_start(rbr[:], rb.to_broadcast([P, 8])).then_inc(sm["ld"], 16)

                @block.vector
                def _(dve):
                    dve.wait_ge(sm["ld"], 64)
                    for i in (0, 2):
                        dve.tensor_scalar(cols[:, i, :], cols[:, i, :], QSCALE, None, ALU.mult).then_inc(sm["setup"], 1)
                    dve.wait_ge(sm["setup"], 2)
            clear()

            T_ATT = (16, 68)
            T_RES = (T_ATT[0] + T_END, T_ATT[1] + T_END)
            T_FFN = T_RES[1] + 7
            T_RES3 = T_FFN + 15
            T_NORM4 = T_RES3 + 5.5
            T_ROUTE = T_NORM4 + 4

            with nc.Fori(0, B // NS) as it:
                with nc.Block() as block:
                    def x_of(sl):
                        return xres[:, bass.ds(it * (NS * TB) + sl.n * TB, TB), :]

                    def ffn_banks(sl):
                        return (sl.dn[1], sl.sc[0], sl.sc[1], sl.dn[0])

                    @block.sync
                    def _(sp):
                        def program(sl):
                            t0 = sl.t0
                            yield t0 - NS * LAG
                            sp.dma_start(sl.ctx_raw[:], ctxT[bass.ds(it * NS + sl.n, 1), :, :].rearrange("o (k p) s -> p (o k) s", p=P)).then_inc(sl.sm["ctx_ld"], 16)
                            yield from sp_mask(sp, sl, 0, mask_dram[bass.ds(it * NS + sl.n, 1)].rearrange("o c g s -> (o c) g s"), t0 + 4)
                            yield from sp_stack(sp, sl, 0, "k", t0 + 8)
                            yield from sp_stack(sp, sl, 0, "q", t0 + 10)
                            yield from sp_stack_max(sp, sl, 0, t0 + T_ATT[0])
                            yield from sp_mask(sp, sl, 1, mask_dram[B].rearrange("c g s -> c g s"), t0 + T_RES[0] + 1)
                            yield from sp_stack(sp, sl, 1, "k", t0 + T_RES[0] + 10)
                            yield from sp_stack(sp, sl, 1, "q", t0 + T_RES[0] + 11)
                            yield from sp_stack_max(sp, sl, 1, t0 + T_ATT[1])
                            yield t0 + T_ROUTE + 1
                            sp.wait_ge(sl.sm["h_ready"], 4)
                            sp.dma_start(xn_t[:, bass.ds(it * (NS * TB) + sl.n * TB, TB), :], sl.h[:]).then_inc(sl.sm["st_x"], 16)
                            yield t0 + T_ROUTE + 8
                            sp.wait_ge(sl.sm["st_x"], 16)
                        side_by_side(*(program(sl) for sl in slots))

                    @block.tensor
                    def _(pe):
                        def program(sl):
                            sm, t0 = sl.sm, sl.t0
                            hT = (sl.hT_hi, sl.hT_lo)
                            yield t0 + 4
                            pe.wait_ge(sm["ctx_split"], 1)
                            pe_project_T(pe, sl.dn[0], CK, (sl.c_hi, sl.c_lo)).then_inc(sm["k_ps"], 1)
                            yield t0 + 5.3
                            pe_project(pe, sl.dn[1], CV, (sl.c_hi, sl.c_lo)).then_inc(sm["v_ps"], 1)
                            yield t0 + 7.5
                            pe.wait_ge(sm["k_split"], 1)
                            yield from pe_h_T(pe, sl, 0, t0 + 7.6)
                            yield t0 + 9.5
                            pe.wait_ge(sm["hT_ready"], 1)
                            pe_project_T(pe, sl.sc[0], CQ, hT).then_inc(sm["q_ps"], 1)
                            yield from pe_attention(pe, sl, 0, t0 + T_ATT[0], CO)
                            yield from pe_h_T(pe, sl, 1, t0 + T_RES[0] + 5)
                            yield t0 + T_RES[0] + 7
                            pe.wait_ge(sm["hT_ready"], 2)
                            pe_project_T(pe, sl.dn[0], SK, hT).then_inc(sm["k_ps"], 1)
                            yield t0 + T_RES[0] + 8
                            pe_project_T(pe, sl.sc[0], SQ, hT).then_inc(sm["q_ps"], 1)
                            yield t0 + T_RES[0] + 9
                            pe_project(pe, sl.dn[1], SV, hT).then_inc(sm["v_ps"], 1)
                            yield from pe_attention(pe, sl, 1, t0 + T_ATT[1], SO)
                            yield from pe_h_T(pe, sl, 2, t0 + T_RES[1] + 5)
                            for j, bank in enumerate(ffn_banks(sl)):
                                yield t0 + T_FFN + 1.4 * j
                                if j == 0:
                                    pe.wait_ge(sm["hT_ready"], 3)
                                for m in (2 * j, 2 * j + 1):
                                    for k in range(KD):
                                        last = mm3(pe, bank[:, (m % 2) * S:(m % 2 + 1) * S], [v[:, k, m * P:(m + 1) * P] for v in fiw],
                                                   [v[:, k, :] for v in hT], k == 0, k == KD - 1)
                                last.then_inc(sm["fc1_ps"], 1)
                            for t in range(TB):
                                for k in range(KF):
                                    yield t0 + T_FFN + (5.7 + k if t == 0 else 13)
                                    if t == 0:
                                        if k == 0:
                                            pe.wait_ge(sm["gelu"], 2)
                                        pe.wait_ge(sm["hid_ready"], k + 1)
                                    last = mm3(pe, sl.dn[1][:, t * D:(t + 1) * D], [v[:, k, t * P:(t + 1) * P] for v in (sl.qstack, sl.kstack)],
                                               [fow[0][:, k, :], fow[1][:, k, :]], k == 0, k == KF - 1)
                            last.then_inc(sm["fc2_ps"], 1)
                            yield from pe_h_T(pe, sl, 3, t0 + T_ROUTE)
                            yield t0 + T_ROUTE + 2.5
                            pe.wait_ge(sm["hT_ready"], 4)
                            for t in range(TB):
                                for k in range(KD):
                                    last = mm3(pe, sl.sc[0][:, t * 8:(t + 1) * 8], [v[:, k, t * P:(t + 1) * P] for v in hT],
                                               [rww[0][:, k, :], rww[1][:, k, :]], k == 0, k == KD - 1)
                            last.then_inc(sm["log_ps"], 1)
                        side_by_side(*(program(sl) for sl in slots))

                    @block.scalar
                    def _(act):
                        def program(sl):
                            sm, t0 = sl.sm, sl.t0
                            yield t0 + 2
                            act.wait_ge(sm["ctx_ld"], 16)
                            act.activation(sl.c_hi, sl.ctx_raw[:], ACT.Copy).then_inc(sm["ctx_hi"], 1)
                            yield from act_qk(act, sl, 0, "k", sl.dn[0], cols[:, 1, :], t0 + 6)
                            yield from act_h_T(act, sl, 0, t0 + 7.6)
                            yield from act_qk(act, sl, 0, "q", sl.sc[0], cols[:, 0, :], t0 + 10.8)
                            yield from act_attention(act, sl, 0, t0 + T_ATT[0])
                            yield from act_h_T(act, sl, 1, t0 + T_RES[0] + 5)
                            yield from act_qk(act, sl, 1, "k", sl.dn[0], cols[:, 3, :], t0 + T_RES[0] + 8.2)
                            yield from act_qk(act, sl, 1, "q", sl.sc[0], cols[:, 2, :], t0 + T_RES[0] + 9.2)
                            yield from act_attention(act, sl, 1, t0 + T_ATT[1])
                            yield from act_h_T(act, sl, 2, t0 + T_RES[1] + 5)
                            g32 = sl.probs[:, 0:KF // TB].rearrange("p a t s -> p (a t) s")
                            for m in range(KF):
                                yield t0 + T_FFN + 1.4 + 0.7 * m
                                act.wait_ge(sm["fc1_ps"], m // 2 + 1)
                                act.activation(g32[:, m, :], ffn_banks(sl)[m // 2][:, (m % 2) * S:(m % 2 + 1) * S], ACT.Gelu,
                                               bias=fibc[:, m:m + 1]).then_inc(sm["gelu"], 1)
                            yield from act_h_T(act, sl, 3, t0 + T_ROUTE)
                        side_by_side(*(program(sl) for sl in slots))

                    @block.gpsimd
                    def _(gp):
                        def program(sl):
                            sm, t0 = sl.sm, sl.t0
                            g32 = sl.probs[:, 0:KF // TB].rearrange("p a t s -> p (a t) s")
                            yield from pool_rstd(gp, sl, 0, t0)
                            yield from pool_ones(gp, sl, t0 + 1.5)
                            for n, (row, t_h) in enumerate(((R_CO, 5), (R_SO, T_RES[0] + 5), (R_FO, T_RES[1] + 5))):
                                yield t0 + t_h
                                gp.wait_ge(sm["h_ready"], n + 1)
                                gp.tensor_tensor(sl.resb[:], sl.h[:], rows[:, row, :].unsqueeze(1).to_broadcast([P, TB, D]), ALU.add).then_inc(sm["resb_ready"], 1)
                                if n == 2:
                                    for m in range(KF):
                                        yield t0 + T_FFN + 2 + 0.7 * m
                                        gp.wait_ge(sm["gelu"], m + 1)
                                        gp.tensor_copy(sl.qstack[:, m, :], g32[:, m, :]).then_inc(sm["hid_hi"], 1)
                                yield from pool_rstd(gp, sl, n + 1, t0 + (*T_RES, T_RES3)[n] + 1)
                            yield from pool_rstd(gp, sl, 4, t0 + T_NORM4)
                        side_by_side(*(program(sl) for sl in slots))

                    @block.vector
                    def _(dve):
                        def program(sl):
                            sm, t0 = sl.sm, sl.t0
                            xb = x_of(sl)
                            g32 = sl.probs[:, 0:KF // TB].rearrange("p a t s -> p (a t) s")
                            ch = Chain(dve, sm["chain"])
                            yield from dve_norm(dve, ch, sl, 0, xb, t0)
                            dve_norm_apply(dve, sl, xb, sl.h).then_inc(sm["h_ready"], 1)
                            yield t0 + 2.8
                            dve.wait_ge(sm["ctx_hi"], 1)
                            dve.tensor_tensor(sl.c_lo, sl.ctx_raw[:], sl.c_hi.bitcast(F32), ALU.subtract).then_inc(sm["ctx_split"], 1)
                            yield from dve_qk(dve, sl, 0, "k", sl.dn[0], cols[:, 1, :], t0 + 6.7)
                            yield from dve_v(dve, sl, 0, rows[:, R_CV, :], t0 + 7.2)
                            yield from dve_h_T(dve, sl, 0, t0 + 7.6)
                            yield from dve_qk(dve, sl, 0, "q", sl.sc[0], cols[:, 0, :], t0 + 11.5)
                            for a, (g, be) in enumerate(((R_CG, R_CBE), (R_SG, R_SBE))):
                                if a == 1:
                                    yield from dve_qk(dve, sl, 1, "k", sl.dn[0], cols[:, 3, :], t0 + T_RES[0] + 9)
                                    yield from dve_qk(dve, sl, 1, "q", sl.sc[0], cols[:, 2, :], t0 + T_RES[0] + 10)
                                    yield from dve_v(dve, sl, 1, rows[:, R_SV, :], t0 + T_RES[0] + 10.5)
                                yield from dve_attention(dve, ch, sl, a, t0 + T_ATT[a])
                                yield t0 + T_RES[a]
                                dve.wait_ge(sm["op_ps"], a + 1)
                                dve.wait_ge(sm["resb_ready"], a + 1)
                                ch(dve.tensor_tensor(sl.res[:].rearrange("p t d -> p (t d)"), sl.dn[0][:, :], sl.resb[:].rearrange("p t d -> p (t d)"), ALU.add))
                                yield from dve_norm(dve, ch, sl, a + 1, sl.res, t0 + T_RES[a] + 1)
                                ch(dve_norm_apply(dve, sl, sl.res, sl.norm))
                                dve_affine(dve, ch, sl, rows[:, g, :], rows[:, be, :].unsqueeze(1).to_broadcast([P, TB, D]), sl.h[:]).then_inc(sm["h_ready"], 1)
                                yield from dve_h_T(dve, sl, a + 1, t0 + T_RES[a] + 5)
                            for m in range(KF):
                                yield t0 + T_FFN + 3 + m
                                dve.wait_ge(sm["hid_hi"], m + 1)
                                dve.tensor_tensor(sl.kstack[:, m, :], g32[:, m, :], sl.qstack[:, m, :].bitcast(F32), ALU.subtract).then_inc(sm["hid_ready"], 1)
                            yield t0 + T_RES3
                            dve.wait_ge(sm["fc2_ps"], 1)
                            dve.wait_ge(sm["resb_ready"], 3)
                            ch(dve.tensor_tensor(sl.res[:].rearrange("p t d -> p (t d)"), sl.dn[1][:, :], sl.resb[:].rearrange("p t d -> p (t d)"), ALU.add))
                            yield from dve_norm(dve, ch, sl, 3, sl.res, t0 + T_RES3 + 1)
                            ch(dve_norm_apply(dve, sl, sl.res, sl.norm))
                            ch(dve_affine(dve, ch, sl, rows[:, R_FG, :], rows[:, R_FBE, :].unsqueeze(1).to_broadcast([P, TB, D]), sl.norm[:]))
                            ch(dve.tensor_tensor(xb, xb, sl.norm[:], ALU.add))
                            yield from dve_norm(dve, ch, sl, 4, xb, t0 + T_NORM4)
                            dve_norm_apply(dve, sl, xb, sl.h).then_inc(sm["h_ready"], 1)
                            yield from dve_h_T(dve, sl, 3, t0 + T_ROUTE)
                            yield t0 + T_ROUTE + 4
                            dve.wait_ge(sm["log_ps"], 1)
                            ch(dve.tensor_tensor(lg[:, bass.ds(it * (NS * TB) + sl.n * TB, TB), :], sl.sc[0][:, 0:16].rearrange("p (t e) -> p t e", e=8),
                                                 rbr[:].unsqueeze(1).to_broadcast([P, TB, 8]), ALU.add))
                        side_by_side(*(program(sl) for sl in slots))
                clear()
            scope.pop()

        with ExitStack() as stB:
            scope.append(stB)
            xn = sb("xn", [P, NT, D])
            sh = [P, NT, 8]
            wts = sb("wts", sh)
            rank = sb("rank", sh)
            tmp = sb("tmp", sh)
            rmask = sb("rmask", sh)
            slot = sb("slot", sh)
            valid = sb("valid", sh)
            off = sb("off", sh)
            ebase = sb("ebase", sh)
            red = sb("red", [P, NT])
            tri = sb("tri", [P, P])
            ones = sb("ones", [P, P])
            slf = sb("slf", [P, 2, NT])
            slu = sb("slu", [P, 2, NT], U32)
            wsel = sb("wsel", [P, 2, NT])
            noop = sb("noop", [P, NT])

            def bc(v):
                return v.unsqueeze(2).to_broadcast(sh)

            raw_in = probs2[0].rearrange("p (k n) -> p k n", k=KD)
            raw_out = probs2[1].rearrange("p (k n) -> p k n", k=KF)
            stE = ExitStack()
            scope.append(stE)
            ei = [(sb("ei_hi", [P, KD, F], F32R)[:], sb("ei_lo", [P, KD, F], F32R)[:]),
                  tuple(v[:].rearrange("p g s -> p (g s)").rearrange("p (k n) -> p k n", k=KD) for v in (slots[1].qstack, slots[1].kstack))]
            eo = [(sb(f"eo_hi{n}", [P, KF, D], F32R)[:], sb(f"eo_lo{n}", [P, KF, D], F32R)[:]) for n in range(2)]
            xe = [sb(f"xe{n}", [P, TB, D]) for n in range(2)]
            ye = [sb(f"ye{n}", [P, TB, D]) for n in range(2)]
            E_SEMS = """tok_ld0 tok_ld1 in_ld out_ld w_hi w_lo_pool w_lo_dve""".split()
            sm.update({k: sem(k) for k in E_SEMS})

            def sp_expert_in(sp, e):
                for k in range(KD):
                    sp.dma_start(raw_in[:, k, :], ein[bass.ds(e * D + k * P, P), :]).then_inc(sm["in_ld"], 16)

            def sp_expert_out(sp, e):
                for k in range(2):
                    sp.dma_start(raw_out[:, 4 * k:4 * k + 4, :], eout[bass.ds(e * F + k * 4 * P, 4 * P), :].rearrange("(k p) n -> p k n", p=P)).then_inc(sm["out_ld"], 16)

            def sp_expert_tokens(sp, e, n):
                sp.dma_start(xe[n][:], moe_in[bass.ds(e * CAP, CAP), :].rearrange("(t p) d -> p t d", p=P)).then_inc(sm[f"tok_ld{n}"], 16)

            def act_expert_hi(act, n, r):
                act.wait_ge(sm["in_ld"], 32 * (r + 1))
                act.activation(ei[n][0], raw_in, ACT.Copy).then_inc(sm["w_hi"], 1)
                act.wait_ge(sm["out_ld"], 32 * (r + 1))
                if r:
                    act.wait_ge(sm["fc2_ps"], r)
                act.activation(eo[n][0], raw_out, ACT.Copy).then_inc(sm["w_hi"], 1)

            def expert_lo(eng, n, r, done, parts):
                for c, (name, raw, w) in enumerate((("in", raw_in, ei), ("out", raw_out, eo))):
                    eng.wait_ge(sm[f"{name}_ld"], 32 * (r + 1))
                    eng.wait_ge(sm["w_hi"], 2 * r + c + 1)
                    half_k = raw.shape[1] // 2
                    k = slice(parts[0] * half_k, parts[1] * half_k)
                    eng.tensor_tensor(w[n][1][:, k, :], raw[:, k, :], w[n][0][:, k, :].bitcast(F32), ALU.subtract).then_inc(sm[done], 1)

            with nc.Block() as block:
                @block.sync
                def _(sp):
                    sp_expert_in(sp, 0)
                    sp_expert_out(sp, 0)
                    sp.wait_ge(sm["scat"], 16 * 2 * NT)
                    sp_expert_tokens(sp, 0, 0)
                    sp.wait_ge(sm["tok_ld0"], 16)

                @block.gpsimd
                def _(gp):
                    gp.memset(tri[:], 1.0).then_inc(sm["pchain"], 1)
                    gp.memset(ones[:], 1.0)
                    gp.wait_ge(sm["pchain"], 1)
                    gp.affine_select(out=tri[:], in_=tri[:], compare_op=ALU.is_ge, fill=0.0, base=0, pattern=[[1, P]], channel_multiplier=-1)
                    gp.iota(ebase[:], pattern=[[0, NT], [CAP, 8]], base=-1 - NE * CAP, channel_multiplier=0,
                            allow_small_or_imprecise_dtypes=True).then_inc(sm["setup"], 1)
                    expert_lo(gp, 0, 0, "w_lo_pool", (0, 2))
                    gp.wait_ge(sm["ld"], 16)
                    gp.wait_ge(sm["route_i"], 1)
                    for t in range(NT):
                        for r in range(2):
                            gp.indirect_dma_start(moe_in, bass.IndirectOffsetOnAxis(ap=slu[:, r, t:t + 1], axis=0), xn[:, t, :], None,
                                                  bounds_check=NE * CAP - 1, oob_is_err=False).then_inc(sm["scat"], 16)
                    gp.wait_ge(sm["scat"], 16 * 2 * NT)

                @block.scalar
                def _(act):
                    act.dma_start(xn[:], xn_t).then_inc(sm["ld"], 16)
                    act.wait_ge(sm["route_e"], 1)
                    act.activation(wts[:], tmp[:], ACT.Exp).then_inc(sm["sig_e"], 1)
                    act_expert_hi(act, 0, 0)

                @block.tensor
                def _(pe):
                    pe.wait_ge(sm["route_m"], 1)
                    pe.wait_ge(sm["setup"], 1)
                    m2 = rmask[:].rearrange("p t e -> p (t e)")
                    pe.matmul(dn[0][:, 0:P], tri[:], m2, start=True, stop=True)
                    pe.matmul(dn[1][:, 0:P], ones[:], m2, start=True, stop=True).then_inc(sm["cum_ps"], 1)

                @block.vector
                def _(dve):
                    ch = Chain(dve, sm["chain"])
                    ch(dve.tensor_reduce(red[:], lg[:], AX.X, ALU.max))
                    dve.tensor_tensor(tmp[:], lg[:], bc(red[:]), ALU.subtract).then_inc(sm["route_e"], 1)
                    dve.wait_ge(sm["sig_e"], 1)
                    ch(dve.tensor_reduce(red[:], wts[:], AX.X, ALU.add))
                    ch(dve.reciprocal(red[:], red[:]))
                    ch(dve.tensor_tensor(wts[:], wts[:], bc(red[:]), ALU.mult))
                    ch(dve.memset(rank[:], 0.0))
                    for e in range(8):
                        ch(dve.tensor_tensor(tmp[:], bc(wts[:, :, e]), wts[:], ALU.is_gt))
                        ch(dve.tensor_tensor(rank[:], rank[:], tmp[:], ALU.add))
                        if e < 7:
                            tail = [P, NT, 7 - e]
                            ch(dve.tensor_tensor(tmp[:, :, e + 1:8], wts[:, :, e].unsqueeze(2).to_broadcast(tail), wts[:, :, e + 1:8], ALU.is_equal))
                            ch(dve.tensor_tensor(rank[:, :, e + 1:8], rank[:, :, e + 1:8], tmp[:, :, e + 1:8], ALU.add))
                    ch(dve.tensor_scalar(tmp[:], rank[:], 2.0, None, ALU.is_lt))
                    dve.scalar_tensor_tensor(rmask[:], wts[:], 0.0, tmp[:], ALU.is_gt, ALU.mult).then_inc(sm["route_m"], 1)
                    dve.wait_ge(sm["cum_ps"], 1)
                    ch(dve.memset(off[:, 0, :], 0.0))
                    for t in range(1, NT):
                        ch(dve.tensor_tensor(off[:, t, :], off[:, t - 1, :], dn[1][:, 8 * (t - 1):8 * t], ALU.add))
                    ch(dve.tensor_tensor(slot[:], off[:], dn[0][:, 0:P].rearrange("p (t e) -> p t e", e=8), ALU.add))
                    ch(dve.scalar_tensor_tensor(valid[:], slot[:], float(CAP), rmask[:], ALU.is_le, ALU.mult))
                    ch(dve.memset(valid[:, :, 7], 0.0))
                    ch(dve.tensor_tensor(noop[:], wts[:, :, 7], rmask[:, :, 7], ALU.mult))
                    dve.wait_ge(sm["setup"], 1)
                    ch(dve.tensor_tensor(slot[:], slot[:], ebase[:], ALU.add))
                    for r in range(2):
                        ch(dve.scalar_tensor_tensor(tmp[:], rank[:], float(r), valid[:], ALU.is_equal, ALU.mult))
                        ch(dve.tensor_tensor(off[:], tmp[:], wts[:], ALU.mult))
                        ch(dve.tensor_reduce(wsel[:, r, :], off[:], AX.X, ALU.add))
                        ch(dve.tensor_tensor(off[:], tmp[:], slot[:], ALU.mult))
                        ch(dve.tensor_reduce(slf[:, r, :], off[:], AX.X, ALU.add))
                    ch(dve.tensor_scalar(slf[:], slf[:], float(NE * CAP), None, ALU.add))
                    dve.tensor_copy(slu[:], slf[:]).then_inc(sm["route_i"], 1)
            clear()

            FC1_BANKS, e_hi, e_lo = banks[2:6], slots[0].qstack, slots[0].kstack

            def experts(first, pair):
                count = 2 if pair else 1
                with nc.Block() as block:
                    @block.sync
                    def _(sp):
                        if pair:
                            sp_expert_tokens(sp, first + 1, 1)
                            sp_expert_in(sp, first + 1)
                            sp_expert_out(sp, first + 1)
                            sp.wait_ge(sm["hT_ps"], 1)
                            sp_expert_tokens(sp, first + 2, 0)
                            for c, load in enumerate((sp_expert_in, sp_expert_out)):
                                sp.wait_ge(sm["w_lo_pool"], c + 1)
                                sp.wait_ge(sm["w_lo_dve"], c + 1)
                                load(sp, first + 2)
                        for n in range(count):
                            sp.wait_ge(sm["y_ready"], n + 1)
                            sp.dma_start(moe_out[bass.ds((first + n) * CAP, CAP), :].rearrange("(t p) d -> p t d", p=P), ye[n][:]).then_inc(sm["st_x"], 16)
                        sp.wait_ge(sm["st_x"], 16 * count)
                        if pair:
                            sp.wait_ge(sm["tok_ld0"], 16)

                    if pair:
                        @block.gpsimd
                        def _(gp):
                            expert_lo(gp, 1, 0, "w_lo_pool", (0, 1))
                            expert_lo(gp, 0, 1, "w_lo_pool", (0, 1))

                    @block.tensor
                    def _(pe):
                        pe_transpose(pe, banks[6], xe[0]).then_inc(sm["hT_ps"], 1)
                        for n in range(count):
                            pe.wait_ge(sm["hT_ready"], n + 1)
                            if n == 1:
                                pe.wait_ge(sm["w_lo_pool"], 1)
                                pe.wait_ge(sm["w_lo_dve"], 1)
                            for j, bank in enumerate(FC1_BANKS):
                                for m in (2 * j, 2 * j + 1):
                                    for k in range(KD):
                                        last = mm3(pe, bank[:, (m % 2) * S:(m % 2 + 1) * S], [v[:, k, m * P:(m + 1) * P] for v in ei[n]],
                                                   [slots[n].hT_hi[:, k, :], slots[n].hT_lo[:, k, :]], k == 0, k == KD - 1)
                                last.then_inc(sm["fc1_ps"], 1)
                            if n + 1 < count:
                                pe.wait_ge(sm["tok_ld1"], 16)
                                pe_transpose(pe, banks[7], xe[1]).then_inc(sm["hT_ps"], 1)
                            if n == 1:
                                pe.wait_ge(sm["w_lo_pool"], 2)
                                pe.wait_ge(sm["w_lo_dve"], 2)
                            for t in range(TB):
                                for k in range(KF):
                                    if t == 0 and k % 2 == 0:
                                        pe.wait_ge(sm["hid_ready"], 4 * n + k // 2 + 1)
                                    last = mm3(pe, banks[n][:, t * D:(t + 1) * D], [e_hi[:, k, t * P:(t + 1) * P], e_lo[:, k, t * P:(t + 1) * P]],
                                               [eo[n][0][:, k, :], eo[n][1][:, k, :]], k == 0, k == KF - 1)
                            last.then_inc(sm["fc2_ps"], 1)

                    def act_tokens_hi(act, n):
                        act.wait_ge(sm["hT_ps"], n + 1)
                        act.activation(slots[n].hT_hi[:].rearrange("p k s -> p (k s)"), banks[6 + n][:, :], ACT.Copy).then_inc(sm["hT_hi_s"], 1)

                    def dve_tokens_lo(dve, n):
                        dve.wait_ge(sm["hT_hi_s"], n + 1)
                        dve.tensor_tensor(slots[n].hT_lo[:].rearrange("p k s -> p (k s)"), banks[6 + n][:, :],
                                          slots[n].hT_hi[:].rearrange("p k s -> p (k s)").bitcast(F32), ALU.subtract).then_inc(sm["hT_ready"], 1)

                    @block.scalar
                    def _(act):
                        act_tokens_hi(act, 0)
                        for n in range(count):
                            for j, bank in enumerate(FC1_BANKS):
                                act.wait_ge(sm["fc1_ps"], 4 * n + j + 1)
                                act.activation(e_hi[:, 2 * j:2 * j + 2, :].rearrange("p k s -> p (k s)"), bank[:, :], ACT.Relu).then_inc(sm["hid_hi"], 1)
                            if n == 0 and pair:
                                act_tokens_hi(act, 1)
                                act_expert_hi(act, 1, 0)
                            if n == 1:
                                act_expert_hi(act, 0, 1)

                    @block.vector
                    def _(dve):
                        dve_tokens_lo(dve, 0)
                        for n in range(count):
                            for j, bank in enumerate(FC1_BANKS):
                                dve.wait_ge(sm["hid_hi"], 4 * n + j + 1)
                                dve.scalar_tensor_tensor(e_lo[:, 2 * j:2 * j + 2, :].rearrange("p k s -> p (k s)"), bank[:, :], 0.0,
                                                         e_hi[:, 2 * j:2 * j + 2, :].rearrange("p k s -> p (k s)").bitcast(F32), ALU.max, ALU.subtract).then_inc(sm["hid_ready"], 1)
                            if n == 0 and pair:
                                dve_tokens_lo(dve, 1)
                                expert_lo(dve, 1, 0, "w_lo_dve", (1, 2))
                            if n == 1:
                                expert_lo(dve, 0, 1, "w_lo_dve", (1, 2))
                            dve.wait_ge(sm["fc2_ps"], n + 1)
                            dve.tensor_copy(ye[n][:].rearrange("p t d -> p (t d)"), banks[n][:, :]).then_inc(sm["y_ready"], 1)
                clear()

            with nc.Fori(0, NE // 2) as pair_no:
                experts(pair_no * 2, True)
            experts(NE - 1, False)
            for k in E_SEMS:
                del sm[k]
            scope.pop()
            stE.close()

            with ExitStack() as stG:
                scope.append(stG)
                gat = sb("gat", [P, NT, 2, D])
                landed = [sem(f"landed{t}") for t in range(NT)]
                with nc.Block() as block:
                    @block.gpsimd
                    def _(gp):
                        for t in range(NT):
                            for r in range(2):
                                gp.indirect_dma_start(gat[:, t, r, :], None, moe_out, bass.IndirectOffsetOnAxis(ap=slu[:, r, t:t + 1], axis=0),
                                                      bounds_check=NE * CAP, oob_is_err=False).then_inc(landed[t], 16)

                    @block.vector
                    def _(dve):
                        for t in range(NT):
                            dve.scalar_tensor_tensor(xres[:, t, :], xn[:, t, :], noop[:, t:t + 1], xres[:, t, :], ALU.mult, ALU.add).then_inc(sm["chain"], 1)
                        for r in range(2):
                            for t in range(NT):
                                dve.wait_ge(sm["chain"], NT * r + t + 1)
                                if r == 0:
                                    dve.wait_ge(landed[t], 32)
                                dve.scalar_tensor_tensor(xres[:, t, :], gat[:, t, r, :], wsel[:, r, t:t + 1], xres[:, t, :], ALU.mult, ALU.add).then_inc(sm["chain"], 1)
                        dve.wait_ge(sm["chain"], 3 * NT)
                clear()
                for s in landed:
                    nc.gpsimd.sem_clear(s)
                nc.all_engine_barrier()
                scope.pop()
            scope.pop()

        with ExitStack() as stC:
            scope.append(stC)
            wq = [(sb(f"wC_hi{i}", [P, KD, D], F32R), sb(f"wC_lo{i}", [P, KD, D], F32R)) for i in range(4)]
            w1w = (sb("w1_hi", [P, KD, F], F32R), sb("w1_lo", [P, KD, F], F32R))
            w2w = (sb("w2_hi", [P, KF, D], F32R), sb("w2_lo", [P, KF, D], F32R))
            load_split([(wC[i].rearrange("(k p) n -> p k n", p=P), wq[i][0][:], wq[i][1][:], QSCALE if i == 0 else 1.0) for i in range(4)]
                       + [(w1.rearrange("(k p) n -> p k n", p=P), w1w[0][:], w1w[1][:], 1.0),
                          (w2.rearrange("(k p) n -> p k n", p=P), w2w[0][:], w2w[1][:], 1.0)])
            LQ, LK, LV, LO = wq
            rows = sb("rowsC", [P, 4, D])
            cols = sb("colsC", [P, 2, KD])
            b1c = sb("b1c", [P, KF])
            infront = sb("infront", [P, TB, S])
            slot_no = sb("slot_no", [P, P])
            for sl in slots:
                def b(name, shape, dt=F32):
                    return sb(f"{name}_{sl.n}", shape, dt)

                sl.sm.update({k: sem(f"{k}_{sl.n}") for k in LATE_SEMS})
                sl.g32 = sl.probs[:, 0:KF * K_SELECT // (TB * S)].rearrange("p a t (c s) -> p (a t c) s", s=K_SELECT)
                sl.g_hi, sl.g_lo = (v[:, 0:HG // 2, :].rearrange("p g (c s) -> p (g c) s", s=K_SELECT) for v in (sl.qstack, sl.kstack))
                sl.hn = b("hn", [P, TB, D])
                sl.score = b("score", [P, TB])
                sl.sig = b("sig", [P, TB])
                sl.spread = sl.resb[:, :, 0:P]
                sl.srow = b("srow", [P, S])
                sl.cmp = b("cmp", [P, S])
                sl.above = b("above", [P, TB, 2])
                sl.trank = b("trank", [P, TB])
                sl.oh = b("oh", [P, TB, P])
                sl.ohT = b("ohT", [P, TB, P])
                sl.proc = b("proc", [P, D])

            with nc.Block() as block:
                @block.sync
                def _(sp):
                    sp.dma_start(rows[:], rowC.unsqueeze(0).to_broadcast([P, 4, D])).then_inc(sm["ld"], 16)
                    sp.dma_start(cols[:], colC).then_inc(sm["ld"], 16)
                    sp.dma_start(b1c[:], b1).then_inc(sm["ld"], 16)

                @block.gpsimd
                def _(gp):
                    gp.memset(infront[:], 1.0).then_inc(sm["pchain"], 1)
                    gp.wait_ge(sm["pchain"], 1)
                    gp.affine_select(out=infront[:], in_=infront[:], compare_op=ALU.is_gt, fill=0.0, base=0, pattern=[[P, TB], [-1, S]], channel_multiplier=1)
                    gp.iota(slot_no[:], pattern=[[1, P]], base=0, channel_multiplier=0, allow_small_or_imprecise_dtypes=True)

                @block.vector
                def _(dve):
                    dve.wait_ge(sm["ld"], 48)
                    dve.tensor_scalar(cols[:, 0, :], cols[:, 0, :], QSCALE, None, ALU.mult).then_inc(sm["setup"], 1)
                    dve.wait_ge(sm["setup"], 1)
            clear()

            T_ATT1 = 16
            T_RES1 = T_ATT1 + T_END
            T_PICK = T_RES1 + 6
            T_FF = T_PICK + 9
            T_LAST = T_FF + 11

            with nc.Fori(0, B // NS) as it:
                with nc.Block() as block:
                    def x_of(sl):
                        return xres[:, bass.ds(it * (NS * TB) + sl.n * TB, TB), :]

                    @block.sync
                    def _(sp):
                        def program(sl):
                            sm, t0 = sl.sm, sl.t0
                            yield t0 - NS * LAG
                            sp.dma_start(sl.ctx_raw[:], ctxT[bass.ds(it * NS + sl.n, 1), :, :].rearrange("o (k p) s -> p (o k) s", p=P)).then_inc(sm["ctx_ld"], 16)
                            yield from sp_mask(sp, sl, 0, mask_dram[B], t0 + 4)
                            yield from sp_stack(sp, sl, 0, "k", t0 + 8)
                            yield from sp_stack(sp, sl, 0, "q", t0 + 12)
                            yield from sp_stack_max(sp, sl, 0, t0 + T_ATT1)
                            yield t0 + T_LAST + 3
                            sp.wait_ge(sm["x_out"], 2)
                            sp.dma_start(out_t[:, bass.ds(it * (NS * TB) + sl.n * TB, TB), :], sl.res[:]).then_inc(sm["st_out"], 16)
                            yield t0 + T_LAST + 10
                            sp.wait_ge(sm["st_out"], 16)
                        side_by_side(*(program(sl) for sl in slots))

                    @block.tensor
                    def _(pe):
                        def program(sl):
                            sm, t0, sc, dn = sl.sm, sl.t0, sl.sc, sl.dn
                            hT = (sl.hT_hi, sl.hT_lo)
                            yield t0 + 4
                            pe.wait_ge(sm["ctx_split"], 1)
                            pe_project_T(pe, dn[0], LK, (sl.c_hi, sl.c_lo)).then_inc(sm["k_ps"], 1)
                            yield t0 + 5.3
                            pe_project(pe, dn[1], LV, (sl.c_hi, sl.c_lo)).then_inc(sm["v_ps"], 1)
                            yield t0 + 7.5
                            pe.wait_ge(sm["k_split"], 1)
                            yield from pe_h_T(pe, sl, 0, t0 + 7.6)
                            yield t0 + 9.5
                            pe.wait_ge(sm["hT_ready"], 1)
                            pe_project_T(pe, sc[0], LQ, hT).then_inc(sm["q_ps"], 1)
                            yield from pe_attention(pe, sl, 0, t0 + T_ATT1, LO)
                            yield t0 + T_PICK
                            pe.wait_ge(sm["route_e"], 1)
                            for t in range(TB):
                                last = pe.transpose(dn[1][:, t * P:(t + 1) * P], sl.spread[:, t, :], ident[:])
                            last.then_inc(sm["srow_ps"], 1)
                            yield t0 + T_PICK + 4
                            pe.wait_ge(sm["onehot"], 1)
                            for k in range(KD):
                                for t in range(TB):
                                    last = pe.matmul(dn[0][:, k * P:(k + 1) * P], sl.hn[:, t, k * P:(k + 1) * P], sl.oh[:, t, :], start=(t == 0), stop=(t == TB - 1))
                            last.then_inc(sm["sel_ps"], 1)
                            yield t0 + T_PICK + 5
                            for t in range(TB):
                                last = pe.transpose(sc[0][:, t * P:(t + 1) * P], sl.oh[:, t, :], ident[:])
                            last.then_inc(sm["ohT_ps"], 1)
                            for j, bank in enumerate((sc[1], dn[1])):
                                yield t0 + T_FF + 2.6 * j
                                if j == 0:
                                    pe.wait_ge(sm["selT_ready"], 1)
                                for m in range(4 * j, 4 * j + 4):
                                    for k in range(KD):
                                        last = mm3(pe, bank[:, (m % 4) * P:(m % 4 + 1) * P], [v[:, k, m * P:(m + 1) * P] for v in w1w],
                                                   [v[:, k, 0:K_SELECT] for v in hT], k == 0, k == KD - 1)
                                last.then_inc(sm["fc1_ps"], 1)
                            for k in range(KF):
                                yield t0 + T_FF + 5 + 0.7 * k
                                pe.wait_ge(sm["hid_ready"], k + 1)
                                last = mm3(pe, dn[0][:, 0:D], [sl.g_hi[:, k, :], sl.g_lo[:, k, :]], [w2w[0][:, k, :], w2w[1][:, k, :]], k == 0, k == KF - 1)
                            last.then_inc(sm["fc2_ps"], 1)
                            yield t0 + T_LAST + 0.8
                            pe.wait_ge(sm["proc_ready"], 1)
                            pe.wait_ge(sm["ohT_ready"], 1)
                            for t in range(TB):
                                last = pe.matmul(sc[1][:, t * D:(t + 1) * D], sl.ohT[:, t, :], sl.proc[:], start=True, stop=True)
                            last.then_inc(sm["upd_ps"], 1)
                        side_by_side(*(program(sl) for sl in slots))

                    @block.scalar
                    def _(act):
                        def program(sl):
                            sm, t0, sc, dn = sl.sm, sl.t0, sl.sc, sl.dn
                            yield t0 + 2
                            act.wait_ge(sm["ctx_ld"], 16)
                            act.activation(sl.c_hi, sl.ctx_raw[:], ACT.Copy).then_inc(sm["ctx_hi"], 1)
                            yield from act_qk(act, sl, 0, "k", dn[0], cols[:, 1, :], t0 + 6)
                            yield from act_h_T(act, sl, 0, t0 + 7.6)
                            yield from act_qk(act, sl, 0, "q", sc[0], cols[:, 0, :], t0 + 10.8)
                            yield from act_attention(act, sl, 0, t0 + T_ATT1)
                            yield t0 + T_PICK
                            act.wait_ge(sm["route_e"], 1)
                            act.activation(sl.sig[:], sl.score[:], ACT.Exp, scale=-1.0).then_inc(sm["sig_e"], 1)
                            yield t0 + T_PICK + 6
                            act.wait_ge(sm["ohT_ps"], 1)
                            act.activation(sl.ohT[:].rearrange("p t s -> p (t s)"), sc[0][:, 0:TB * P], ACT.Copy).then_inc(sm["ohT_ready"], 1)
                            for m in range(KF):
                                yield t0 + T_FF + 2.6 + 0.5 * m
                                act.wait_ge(sm["fc1_ps"], m // 4 + 1)
                                act.activation(sl.g32[:, m, :], (sc[1], dn[1])[m // 4][:, (m % 4) * P:(m % 4 + 1) * P], ACT.Gelu_apprx_tanh, bias=b1c[:, m:m + 1]).then_inc(sm["gelu"], 1)
                        side_by_side(*(program(sl) for sl in slots))

                    @block.gpsimd
                    def _(gp):
                        def program(sl):
                            sm, t0 = sl.sm, sl.t0
                            yield from pool_rstd(gp, sl, 0, t0)
                            yield from pool_ones(gp, sl, t0 + 1.5)
                            yield t0 + 5
                            gp.tensor_tensor(sl.resb[:], x_of(sl), rows[:, R_LO, :].unsqueeze(1).to_broadcast([P, TB, D]), ALU.add).then_inc(sm["resb_ready"], 1)
                            yield from pool_rstd(gp, sl, 1, t0 + T_RES1 + 1)
                            for m in range(KF):
                                yield t0 + T_FF + 3.2 + 0.5 * m
                                gp.wait_ge(sm["gelu"], m + 1)
                                gp.tensor_copy(sl.g_hi[:, m, :], sl.g32[:, m, :]).then_inc(sm["hid_hi"], 1)
                        side_by_side(*(program(sl) for sl in slots))

                    @block.vector
                    def _(dve):
                        def program(sl):
                            sm, t0, sc, dn = sl.sm, sl.t0, sl.sc, sl.dn
                            xb = x_of(sl)
                            ch = Chain(dve, sm["chain"])
                            yield from dve_norm(dve, ch, sl, 0, xb, t0)
                            dve_norm_apply(dve, sl, xb, sl.h).then_inc(sm["h_ready"], 1)
                            yield t0 + 2.8
                            dve.wait_ge(sm["ctx_hi"], 1)
                            dve.tensor_tensor(sl.c_lo, sl.ctx_raw[:], sl.c_hi.bitcast(F32), ALU.subtract).then_inc(sm["ctx_split"], 1)
                            yield from dve_qk(dve, sl, 0, "k", dn[0], cols[:, 1, :], t0 + 6.7)
                            yield from dve_v(dve, sl, 0, rows[:, R_LV, :], t0 + 7.2)
                            yield from dve_h_T(dve, sl, 0, t0 + 7.6)
                            yield from dve_qk(dve, sl, 0, "q", sc[0], cols[:, 0, :], t0 + 11.5)
                            yield from dve_attention(dve, ch, sl, 0, t0 + T_ATT1)
                            yield t0 + T_RES1
                            dve.wait_ge(sm["op_ps"], 1)
                            dve.wait_ge(sm["resb_ready"], 1)
                            ch(dve.tensor_tensor(sl.res[:].rearrange("p t d -> p (t d)"), dn[0][:, :], sl.resb[:].rearrange("p t d -> p (t d)"), ALU.add))
                            yield from dve_norm(dve, ch, sl, 1, sl.res, t0 + T_RES1 + 1)
                            ch(dve_norm_apply(dve, sl, sl.res, sl.hn))
                            for t in range(TB):
                                last = dve.tensor_tensor_reduce(sl.norm[:, t, :], sl.hn[:, t, :], rows[:, R_RT, :], 1.0, 0.0, ALU.mult, ALU.add, sl.score[:, t:t + 1])
                            ch(last)
                            dve.tensor_copy(sl.spread, sl.score[:].unsqueeze(2).to_broadcast([P, TB, P])).then_inc(sm["route_e"], 1)
                            ch(dve.tensor_tensor(sl.res[:], sl.res[:], sl.hn[:], ALU.add))
                            yield t0 + T_PICK + 1
                            dve.wait_ge(sm["srow_ps"], 1)
                            ch(dve.tensor_copy(sl.srow[:], dn[1][:, 0:S]))
                            for t in range(TB):
                                ch(dve.tensor_scalar(sl.cmp[:], sl.srow[:], sl.score[:, t:t + 1], None, ALU.is_gt, ALU.add, accum_out=sl.above[:, t, 0:1]))
                                ch(dve.scalar_tensor_tensor(sl.cmp[:], sl.srow[:], sl.score[:, t:t + 1], infront[:, t, :], ALU.is_equal, ALU.mult, accum_out=sl.above[:, t, 1:2]))
                            ch(dve.tensor_tensor(sl.trank[:], sl.above[:, :, 0], sl.above[:, :, 1], ALU.add))
                            for t in range(TB):
                                last = dve.tensor_scalar(sl.oh[:, t, :], slot_no[:], sl.trank[:, t:t + 1], None, ALU.is_equal)
                            last.then_inc(sm["onehot"], 1)
                            yield t0 + T_PICK + 4.5
                            dve.wait_ge(sm["sig_e"], 1)
                            ch(dve.tensor_scalar(sl.sig[:], sl.sig[:], 1.0, None, ALU.add))
                            ch(dve.reciprocal(sl.sig[:], sl.sig[:]))
                            yield t0 + T_PICK + 6
                            dve.wait_ge(sm["sel_ps"], 1)
                            sel = dn[0][:, 0:KD * P].rearrange("p (k s) -> p k s", k=KD)
                            ch(dve.tensor_copy(sl.hT_hi[:, :, 0:K_SELECT], sel))
                            dve.tensor_tensor(sl.hT_lo[:, :, 0:K_SELECT], sel, sl.hT_hi[:, :, 0:K_SELECT].bitcast(F32), ALU.subtract).then_inc(sm["selT_ready"], 1)
                            for m in range(KF):
                                yield t0 + T_FF + 4.3 + 0.7 * m
                                dve.wait_ge(sm["hid_hi"], m + 1)
                                dve.tensor_tensor(sl.g_lo[:, m, :], sl.g32[:, m, :], sl.g_hi[:, m, :].bitcast(F32), ALU.subtract).then_inc(sm["hid_ready"], 1)
                            yield t0 + T_LAST
                            dve.wait_ge(sm["fc2_ps"], 1)
                            dve.tensor_tensor(sl.proc[:], dn[0][:, 0:D], rows[:, R_B2, :], ALU.add).then_inc(sm["proc_ready"], 1)
                            yield t0 + T_LAST + 2
                            dve.wait_ge(sm["upd_ps"], 1)
                            for t in range(TB):
                                dve.scalar_tensor_tensor(sl.res[:, t, :], sc[1][:, t * D:(t + 1) * D], sl.sig[:, t:t + 1], sl.res[:, t, :], ALU.mult, ALU.add).then_inc(sm["x_out"], 1)
                        side_by_side(*(program(sl) for sl in slots))
                clear()
            scope.pop()


def kernel(**inputs):
    import numpy as _np
    import concourse.bacc as _bacc
    from concourse import mybir as _mybir
    from concourse.bass_utils import run_bass_kernel_spmd as _run

    g = {k: _np.asarray(v) for k, v in inputs.items()}

    def head_cols(w):
        return w.reshape(-1, 2, HG, DH).transpose(0, 1, 3, 2).reshape(w.shape)

    def head_col_bias(v):
        return v.reshape(2, HG, DH).transpose(2, 1, 0).reshape(P, 2)

    def col(v):
        return v.reshape(-1, P).T

    a, c = "L0_xattn_", "L1_xattn_"
    data = {
        "x": g["x"].reshape(B * S, D),
        "ctxT": g["ctx_1024"].transpose(0, 2, 1),
        "mask": g["mask_Bx1x1xS2_ff0"].reshape(B, S),
        "wA": _np.stack([head_cols(g[a + "cq_w"]), head_cols(g[a + "ck_w"]), g[a + "cv_w"], g[a + "co_w"],
                         head_cols(g[a + "sq_w"]), head_cols(g[a + "sk_w"]), g[a + "sv_w"], g[a + "so_w"]]),
        "colA": _np.stack([head_col_bias(g[a + n]) for n in ("cq_b", "ck_b", "sq_b", "sk_b")], axis=1),
        "rowA": _np.stack([g[a + n] for n in ("cv_b", "co_b", "co_g", "co_be", "sv_b", "so_b", "so_g", "so_be", "fo_b", "fo_g", "fo_be")]),
        "fi": g[a + "fi_w"], "fo": g[a + "fo_w"], "fib": col(g[a + "fi_b"]),
        "rw": g["L0_ffn_router_w"].T, "rb": g["L0_ffn_router_b"].reshape(1, 8),
        "ein": g["L0_ffn_experts_inter"].reshape(NE * D, F), "eout": g["L0_ffn_experts_out"].reshape(NE * F, D),
        "wC": _np.stack([head_cols(g[c + "W_q"].T), head_cols(g[c + "W_k"].T), g[c + "W_v"].T, g[c + "W_o"].T]),
        "colC": _np.stack([head_col_bias(g[c + n]) for n in ("b_q", "b_k")], axis=1),
        "rowC": _np.stack([g[c + "b_v"], g[c + "b_o"], g["L1_ffn_b2"], g["L1_ffn_w_router"]]),
        "w1": g["L1_ffn_W1"], "w2": g["L1_ffn_W2"], "b1": col(g["L1_ffn_b1"]),
    }
    nc = _bacc.Bacc("TRN2", target_bir_lowering=False, num_devices=1)
    arrays, args = {}, []
    for name, v in data.items():
        v = _np.ascontiguousarray(v)
        arrays[f"in_{name}"] = v
        args.append(nc.dram_tensor(f"in_{name}", v.shape, _mybir.dt.from_np(v.dtype), kind="ExternalInput").ap())
    args.append(nc.dram_tensor("out_0", (B * S, D), F32, kind="ExternalOutput").ap())
    build(nc, *args)
    r = _run(nc, [arrays], core_ids=[0])
    return r.results[0]["out_0"].reshape(B, S, D)
```
